# Optimizing a Trainium2 kernel written in Bass

```python
import numpy as np
import jax
import jax.numpy as jnp

def _softmax(x, axis=-1):
    return jax.nn.softmax(x, axis=axis)

def _gelu(x):
    return jax.nn.gelu(x, approximate=True)

def _silu(x):
    return jax.nn.silu(x)

def _sigmoid(x):
    return jax.nn.sigmoid(x)

def _layernorm(x, axis=-1, eps=1e-05):
    m = jnp.mean(x, axis=axis, keepdims=True)
    v = jnp.var(x, axis=axis, keepdims=True)
    return (x - m) / jnp.sqrt(v + eps)

def _scatter_add(tgt, idx, src, axis=0):
    return tgt.at[idx].add(src)

def _segment_sum(src, seg, n):
    return jax.ops.segment_sum(src, seg, n)
kernel_name = 'mk_adaln_d1_jaxref_r4_6e475c'

def setup_inputs(seed: int=0):
    np.random.seed(seed)
    _w = jnp.asarray

    def _L0_attn_setup():
        import jax, jax.numpy as jnp
        import numpy as np
        import math
        B, T, E, H = (4, 512, 256, 16)
        D = E // H
        rng = jax.random.key(seed)
        k1, k2, k3, k4, k5 = jax.random.split(rng, 5)
        scale_w = 1.0 / math.sqrt(E)
        return {'query': jax.random.normal(k1, (B, T, E), jnp.float32), 'key': jax.random.normal(k2, (B, T, E), jnp.float32), 'value': jax.random.normal(k3, (B, T, E), jnp.float32), 'in_proj_weight': jax.random.normal(k4, (3 * E, E), jnp.float32) * scale_w, 'out_proj_weight': jax.random.normal(k5, (E, E), jnp.float32) * scale_w}
    _L0_attn_in = _L0_attn_setup()

    def _L0_ffn_setup():
        import jax, jax.numpy as jnp
        import numpy as np
        DIM = 256

        def _reference_tuple_inner(x, W_r, W_k, W_v, mu_r, mu_k):
            B, T, C = x.shape
            x_prev = jnp.concatenate([jnp.zeros((B, 1, C), x.dtype), x[:, :-1, :]], axis=1)
            xr = mu_r * x + (1.0 - mu_r) * x_prev
            xk = mu_k * x + (1.0 - mu_k) * x_prev
            r = jax.nn.sigmoid(jnp.einsum('btc,dc->btd', xr, W_r))
            k = jnp.einsum('btc,dc->btd', xk, W_k)
            k_act = jnp.square(jax.nn.relu(k))
            out = r * jnp.einsum('btc,dc->btd', k_act, W_v)
            new_state = x[:, -1, :]
            return (out, new_state)
        key = jax.random.key(seed)
        ks = jax.random.split(key, 6)
        B, T, C = (8, 512, DIM)
        x = jax.random.normal(ks[0], (B, T, C), dtype=jnp.float32)
        s = 1.0 / np.sqrt(C)
        W_r = jax.random.uniform(ks[1], (C, C), jnp.float32, -s, s)
        W_k = jax.random.uniform(ks[2], (C, C), jnp.float32, -s, s)
        W_v = jax.random.uniform(ks[3], (C, C), jnp.float32, -s, s)
        mu_r = jax.random.uniform(ks[4], (C,), jnp.float32)
        mu_k = jax.random.uniform(ks[5], (C,), jnp.float32)
        return {'x': x, 'W_r': W_r, 'W_k': W_k, 'W_v': W_v, 'mu_r': mu_r, 'mu_k': mu_k}
    _L0_ffn_in = _L0_ffn_setup()
    _L0_c = _w((lambda *s: np.random.randn(*s).astype(np.float32) * 0.05)(16, 256))
    _L0_wmod = _w((lambda *s: np.random.randn(*s).astype(np.float32) * 0.05)(256, 6 * 256) * 256 ** (-0.5))
    _d = {'L0_attn_query': _L0_attn_in['query'], 'L0_attn_key': _L0_attn_in['key'], 'L0_attn_value': _L0_attn_in['value'], 'L0_attn_in_proj_weight': _L0_attn_in['in_proj_weight'], 'L0_attn_out_proj_weight': _L0_attn_in['out_proj_weight'], 'L0_ffn_W_r': _L0_ffn_in['W_r'], 'L0_ffn_W_k': _L0_ffn_in['W_k'], 'L0_ffn_W_v': _L0_ffn_in['W_v'], 'L0_ffn_mu_r': _L0_ffn_in['mu_r'], 'L0_ffn_mu_k': _L0_ffn_in['mu_k'], 'L0_c': _L0_c, 'L0_wmod': _L0_wmod}
    _x0 = _d['L0_attn_query']
    _d['L0_attn_query'] = jax.random.normal(jax.random.fold_in(jax.random.key(seed), 1), (16, 512, 256), dtype=_x0.dtype)
    del _x0
    return _d

def reference(L0_attn_query, L0_attn_key, L0_attn_value, L0_attn_in_proj_weight, L0_attn_out_proj_weight, L0_ffn_W_r, L0_ffn_W_k, L0_ffn_W_v, L0_ffn_mu_r, L0_ffn_mu_k, L0_c, L0_wmod):

    def _L0_attn_ref(query, key, value, in_proj_weight, out_proj_weight):
        import jax, jax.numpy as jnp
        import numpy as np
        import math
        B, T, E, H = (4, 512, 256, 16)
        D = E // H
        b, t, e = query.shape
        qkv = jnp.einsum('bte,fe->btf', query, in_proj_weight).reshape(b, t, 3, H, D)
        q = jnp.transpose(qkv[:, :, 0], (0, 2, 1, 3))
        k = jnp.transpose(qkv[:, :, 1], (0, 2, 1, 3))
        v = jnp.transpose(qkv[:, :, 2], (0, 2, 1, 3))
        q = q / math.sqrt(D)
        scores = jnp.einsum('bhqd,bhkd->bhqk', q, k)
        pos = jnp.arange(t)
        causal = pos[:, None] >= pos[None, :]
        scores = jnp.where(causal[None, None], scores, jnp.float32(-jnp.inf))
        attn = jax.nn.softmax(scores, axis=-1)
        out = jnp.einsum('bhqk,bhkd->bhqd', attn, v)
        out = jnp.transpose(out, (0, 2, 1, 3)).reshape(b, t, e)
        out = jnp.einsum('bte,fe->btf', out, out_proj_weight)
        return out

    def _L0_ffn_ref(x, W_r, W_k, W_v, mu_r, mu_k):
        import jax, jax.numpy as jnp
        import numpy as np
        DIM = 256

        def _reference_tuple_inner(x, W_r, W_k, W_v, mu_r, mu_k):
            B, T, C = x.shape
            x_prev = jnp.concatenate([jnp.zeros((B, 1, C), x.dtype), x[:, :-1, :]], axis=1)
            xr = mu_r * x + (1.0 - mu_r) * x_prev
            xk = mu_k * x + (1.0 - mu_k) * x_prev
            r = jax.nn.sigmoid(jnp.einsum('btc,dc->btd', xr, W_r))
            k = jnp.einsum('btc,dc->btd', xk, W_k)
            k_act = jnp.square(jax.nn.relu(k))
            out = r * jnp.einsum('btc,dc->btd', k_act, W_v)
            new_state = x[:, -1, :]
            return (out, new_state)
        return _reference_tuple_inner(x, W_r, W_k, W_v, mu_r, mu_k)[0]
    x = L0_attn_query
    mod = (_silu(L0_c) @ L0_wmod).reshape(L0_c.shape[0], 6, 1, -1)
    sa, ca, ga, sb, cb, gb = (mod[:, 0], mod[:, 1], mod[:, 2], mod[:, 3], mod[:, 4], mod[:, 5])
    ga = (2 * (ga >= 0) - 1) * jnp.maximum(jnp.abs(ga), 0.25)
    gb = (2 * (gb >= 0) - 1) * jnp.maximum(jnp.abs(gb), 0.25)
    h = _layernorm(x, axis=-1) * (1 + ca) + sa
    x = x + ga * _L0_attn_ref(h, L0_attn_key, L0_attn_value, L0_attn_in_proj_weight, L0_attn_out_proj_weight)
    h = _layernorm(x, axis=-1) * (1 + cb) + sb
    x = x + gb * _L0_ffn_ref(h, L0_ffn_W_r, L0_ffn_W_k, L0_ffn_W_v, L0_ffn_mu_r, L0_ffn_mu_k)
    return x

_drawn_inputs = setup_inputs


def setup_inputs(seed=0):
    import zlib

    import numpy as np

    out = dict(_drawn_inputs(seed))
    spreads = {}
    factors = {'L0_ffn_W_r': 8.0,
     'L0_ffn_W_k': 3.019,
     'L0_ffn_W_v': 2.766,
     'L0_ffn_mu_r': 8.0,
     'L0_ffn_mu_k': 5.004}
    for name, (base, spread) in spreads.items():
        noise = np.random.default_rng([zlib.crc32(name.encode()), seed]).standard_normal(out[name].shape)
        drawn = base * np.exp(spread * noise) if base else spread * noise
        out[name] = jnp.asarray(drawn.astype(out[name].dtype))
    for name, factor in factors.items():
        out[name] = (out[name] * factor).astype(out[name].dtype)
    return out
```

```python
import concourse.bass as bass
from concourse import mybir
from contextlib import ExitStack


def adaln_attention_channel_mix_kernel(nc, x, qk_w, v_w, o_w, r_w, k_w, c_w, mu_r, mu_k, cond, mod_w, out):
    f32, bf16, i32 = mybir.dt.float32, mybir.dt.bfloat16, mybir.dt.int32
    ALU, ACT, AX = mybir.AluOpType, mybir.ActivationFunctionType, mybir.AxisListType

    B, T, E = x.shape
    P = 128
    TT = T // P
    EC = E // P
    H, D = 16, 16
    HS = P // D
    SL = H // HS
    HG = 4
    GS = HS // HG
    CT = 32
    NPC = 3
    KQ = 6 * D
    KS = KQ + 2
    RING = 4
    HT = sum(T - kb * P for kb in range(TT))
    SCALE = 1.0 / D ** 0.5
    EPS = 1e-5
    RSQRT_SEED = float(0x5f3759df)
    NEWTON = 3
    STATS_STEPS = 4 + 3 * NEWTON
    NEG = -1e30
    UM = 11
    UE = 10
    KBO = [0, T, 2 * T, T + 384]
    QR, KR = [(0, 3, 0), (3, 2, 0), (5, 1, 0)], [(0, 0), (1, 0), (2, 0), (3, 1), (4, 1), (5, 2)]

    gate_dram = nc.dram_tensor("gate_rows", [B, 2 * E], f32, kind="Internal").ap()
    modc_dram = nc.dram_tensor("mod_columns", [B, P, 8], f32, kind="Internal").ap()
    q_dram = nc.dram_tensor("q_pieces", [RING, NPC, P, T], bf16, kind="Internal").ap()
    k_dram = nc.dram_tensor("k_pieces", [RING, NPC, P, T], bf16, kind="Internal").ap()
    m_dram = nc.dram_tensor("max_pieces", [RING, 2, HS, T], bf16, kind="Internal").ap()

    ctx = ExitStack()
    with ctx:
        def sb(name, shape, dt=f32):
            return ctx.enter_context(nc.sbuf_tensor(name, shape, dt))

        def sem(name):
            return ctx.enter_context(nc.semaphore(name))

        qk_sb = sb("qk_sb", [P, EC, 2 * E])
        v_sb = sb("v_sb", [P, EC, E])
        o_sb = sb("o_sb", [P, EC, E])
        r_sb = sb("r_sb", [P, EC, E])
        k_sb = sb("k_sb", [P, EC, E])
        c_sb = sb("c_sb", [P, EC, E])
        og_sb = sb("og_sb", [P, EC, E])
        cg_sb = sb("cg_sb", [P, EC, E])
        mu_sb = sb("mu_sb", [P, 2, EC])
        gate_sb = sb("gate_sb", [P, 2 * E])
        mpre = sb("mpre", [P, 8])
        mpost = sb("mpost", [P, 8])
        ident = sb("ident", [P, P])
        identb = sb("identb", [P, P], bf16)
        nidentb = sb("nidentb", [P, P], bf16)
        maskb = sb("maskb", [P, P], bf16)
        xin = sb("xin", [P, TT, E])
        st1 = sb("st1", [P, TT, 6])
        mv1 = sb("mv1", [P, TT, 2])
        nwt = sb("nwt", [P, 4, TT])
        rs1 = sb("rs1", [P, TT])
        nm1 = sb("nm1", [P, TT])
        hT = sb("hT", [P, EC, T])
        qsp = sb("qsp", [P, NPC, T], bf16)
        ksp = sb("ksp", [P, NPC, T], bf16)
        Qs = [sb(f"Qs{r}", [KS, HS, T], bf16) for r in range(RING)]
        Ks = [sb(f"Ks{r}", [KS, HS, T], bf16) for r in range(RING)]
        Va = [sb(f"Va{r}", [P, TT, HS, CT]) for r in range(RING)]
        rmax = sb("rmax", [P, TT, HS])
        mT = sb("mT", [HS, 2, T], bf16)
        PT = [sb(f"PT{g}", [P, HG, HT]) for g in range(GS)]
        oT = sb("oT", [P, SL * GS, T])
        pool_mark = sb("pool_mark", [P, 1])
        rec = sb("rec", [P, H])
        attn = sb("attn", [P, TT, E])
        aT = sb("aT", [P, EC, T])
        x1 = sb("x1", [P, TT, E])
        st2 = sb("st2", [P, TT, 6])
        mv2 = sb("mv2", [P, TT, 2])
        rs2 = sb("rs2", [P, TT])
        nm2 = sb("nm2", [P, TT])
        h2 = sb("h2", [P, EC, T + 1])
        xr = sb("xr", [P, EC, T])
        xk = sb("xk", [P, EC, T])
        ka = sb("ka", [P, EC, T])
        y = sb("y", [P, TT, E])
        mod_sb = sb_view(PT[0], P, EC, 6 * E)
        cond_sb = y[:, 0, 0:EC * B].rearrange("p (c b) -> p c b", c=EC)
        th_sb = y[:, 1, 0:EC * B].rearrange("p (c b) -> p c b", c=EC)
        sT = y[:, 2, 0:EC * B].rearrange("p (c b) -> p c b", c=EC)
        gr = [xr[0:B, 0, :], xr[0:B, 1, :], xk[0:B, 0, :], xk[0:B, 1, :]]
        modc = ka[:, 0, 0:B * 8].rearrange("p (b k) -> p b k", k=8)

        def bank(name):
            return ctx.enter_context(nc.psum_tensor(name, [P, 512], f32))

        ES = [bank(f"scores{i}") for i in range(2)]
        MX = [bank(f"maxed{i}") for i in range(2)]
        OT = [bank(f"pv{i}") for i in range(2)]
        PA = bank("pre_bank")
        PB = bank("post_bank")

        weights_loaded = sem("weights_loaded")
        cond_loaded = sem("cond_loaded")
        zeros_ready = sem("zeros_ready")
        ident_ready = sem("ident_ready")
        const_ready = sem("const_ready")
        bf_ready = sem("bf_ready")
        th_ready = sem("th_ready")
        silu_ready = sem("silu_ready")
        modc_full = sem("modc_full")
        modc_ready = sem("modc_ready")
        gate_full = sem("gate_full")
        gate_step = sem("gate_step")
        gate_ready = sem("gate_ready")
        mod_stored = sem("mod_stored")
        x_loaded = sem("x_loaded")
        mpre_loaded = sem("mpre_loaded")
        stats1_step = sem("stats1_step")
        rstd1_ready = sem("rstd1_ready")
        xn1_ready = sem("xn1_ready")
        xnT_full = sem("xnT_full")
        hT_done = sem("hT_done")
        q_full = sem("q_full")
        q_piece = sem("q_piece")
        k_full = sem("k_full")
        k_piece = sem("k_piece")
        v_full = sem("v_full")
        v_done = sem("v_done")
        q_stored = sem("q_stored")
        k_stored = sem("k_stored")
        stack_loaded = sem("stack_loaded")
        max_full = sem("max_full")
        max_read = sem("max_read")
        mT_full = sem("mT_full")
        m1_ready = sem("m1_ready")
        m2_ready = sem("m2_ready")
        m_stored = sem("m_stored")
        m_loaded = sem("m_loaded")
        sc_full = sem("sc_full")
        exp_done = sem("exp_done")
        masked = sem("masked")
        pv_full = sem("pv_full")
        oT_done = sem("oT_done")
        post_loaded = sem("post_loaded")
        gates_folded = sem("gates_folded")
        oTT_full = sem("oTT_full")
        rec_ready = sem("rec_ready")
        attn_done = sem("attn_done")
        aT_full = sem("aT_full")
        aT_done = sem("aT_done")
        o_full = sem("o_full")
        x1_done = sem("x1_done")
        stats2_step = sem("stats2_step")
        rstd2_ready = sem("rstd2_ready")
        xn2_ready = sem("xn2_ready")
        xn2T_full = sem("xn2T_full")
        h2_done = sem("h2_done")
        diff_done = sem("diff_done")
        mixed = sem("mixed")
        kp_full = sem("kp_full")
        relu_done = sem("relu_done")
        act_done = sem("act_done")
        rp_full = sem("rp_full")
        tanh_done = sem("tanh_done")
        vp_full = sem("vp_full")
        y_done = sem("y_done")
        out_added = sem("out_added")
        out_stored = sem("out_stored")

        block = ctx.enter_context(nc.Block())

        def later(count):
            return not isinstance(count, int) or count > 0

        def slots(e, prologue, half, epilogue):
            prologue()
            for i in range(SL):
                half(0, 0, i, True, False)
            with e.Fori(0, (B - 2) // 2) as pair:
                for k in range(2):
                    for i in range(SL):
                        half(2 * pair + 1 + k, (1 + k) % 2, i, False, False)
            for i in range(SL):
                half(B - 1, (B - 1) % 2, i, False, True)
            epilogue()

        def ring(par, i):
            return SL * par + i

        @block.sync
        def _(sp):
            sp.dma_start(xin[:, :, :], x[0].rearrange("(t p) e -> p t e", p=P)).then_inc(x_loaded, 16)
            sp.dma_start(cond_sb, cond.rearrange("(c p) b -> p c b", p=P)).then_inc(cond_loaded, 16)
            sp.dma_start(mod_sb, mod_w.rearrange("(c p) f -> p c f", p=P)).then_inc(cond_loaded, 16)
            for dst, src in ((qk_sb, qk_w), (v_sb, v_w), (o_sb, o_w), (r_sb, r_w), (k_sb, k_w), (c_sb, c_w)):
                sp.dma_start(dst[:, :, :], src.rearrange("(c p) f -> p c f", p=P)).then_inc(weights_loaded, 16)
            sp.dma_start(mu_sb[:, 0, :], mu_r).then_inc(weights_loaded, 16)
            sp.dma_start(mu_sb[:, 1, :], mu_k).then_inc(weights_loaded, 16)
            sp.wait_ge(modc_ready, 2)
            sp.dma_start(modc_dram.rearrange("b p k -> p b k"), modc).then_inc(mod_stored, 16)
            sp.wait_ge(gate_ready, 1)
            sp.dma_start(gate_dram, gr[3]).then_inc(mod_stored, 16)
            sp.wait_ge(mod_stored, 32)

            def load_mpre(b):
                if later(EC * b):
                    sp.wait_ge(hT_done, EC * b)
                sp.dma_start(mpre[:, :], modc_dram[b]).then_inc(mpre_loaded, 16)

            def load_x(b):
                if later(EC * b):
                    sp.wait_ge(xnT_full, EC * b)
                sp.dma_start(xin[:, :, :], x[b].rearrange("(t p) e -> p t e", p=P)).then_inc(x_loaded, 16)
                load_mpre(b)

            def stack(n, r):
                sp.wait_ge(q_piece, NPC * (n + 1))
                sp.dma_start(q_dram[r].rearrange("a p q -> p a q"), qsp[:, :, :]).then_inc(q_stored, 16)
                sp.wait_ge(k_piece, NPC * (n + 1))
                sp.dma_start(k_dram[r].rearrange("a p q -> p a q"), ksp[:, :, :]).then_inc(k_stored, 16)
                sp.wait_ge(q_stored, 16 * (n + 1))
                for j, cnt, a in QR:
                    src = q_dram[r, a:a + cnt].rearrange("a (d h) q -> (a d) (h q)", h=HS)
                    sp.dma_start(Qs[r][D * j:D * (j + cnt), :, :].rearrange("p h q -> p (h q)"), src)\
                      .then_inc(stack_loaded, 16)
                sp.wait_ge(k_stored, 16 * (n + 1))
                for j, a in KR:
                    src = k_dram[r, a].rearrange("(d h) q -> d (h q)", h=HS)
                    sp.dma_start(Ks[r][D * j:D * (j + 1), :, :].rearrange("p h q -> p (h q)"), src)\
                      .then_inc(stack_loaded, 16)

            def max_rows(n, r):
                sp.wait_ge(m2_ready, n + 1)
                sp.dma_start(m_dram[r].rearrange("a h q -> h a q"), mT[:, :, :]).then_inc(m_stored, 16)
                sp.wait_ge(m_stored, 16 * (n + 1))
                sp.dma_start(Qs[r][KQ:KS, :, :].rearrange("p h q -> p (h q)"),
                             m_dram[r].rearrange("a h q -> a (h q)")).then_inc(m_loaded, 16)

            def post_loads(b):
                if later(b):
                    sp.wait_ge(out_added, b)
                sp.dma_start(gate_sb[:, :], bcast_rows(gate_dram, b, P)).then_inc(post_loaded, 16)
                sp.dma_start(mpost[:, :], modc_dram[b]).then_inc(post_loaded, 16)
                sp.dma_start(x1[:, :, :], x[b].rearrange("(t p) e -> p t e", p=P)).then_inc(post_loaded, 16)

            def prologue():
                load_mpre(0)
                stack(0, 0)
                sp.wait_ge(stack_loaded, 16 * (len(QR) + len(KR)))
                stack(1, 1)
                max_rows(0, 0)

            def half(b, par, i, first, last):
                n = SL * b + i
                if i == 0:
                    if not last:
                        load_x(b + 1)
                    if not first:
                        post_loads(b - 1)
                if not last:
                    stack(n + 2, ring(1 - par, i))
                if i == 0:
                    max_rows(n + 1, ring(par, 1))
                elif not last:
                    max_rows(n + 1, ring(1 - par, 0))

            def epilogue():
                post_loads(B - 1)

            slots(sp, prologue, half, epilogue)
            sp.wait_ge(out_stored, 16 * B)

        @block.tensor
        def _(pe):
            mm = nc.tensor.matmul

            pe.wait_ge(cond_loaded, 32)
            pe.wait_ge(silu_ready, 1)
            for k, blk in enumerate((0, 1, 3, 4)):
                for co in range(EC):
                    for c in range(EC):
                        last = mm(PA[:, (EC * k + co) * B:(EC * k + co + 1) * B],
                                  mod_sb[:, c, blk * E + co * P:blk * E + (co + 1) * P], sT[:, c, :],
                                  start=(c == 0), stop=(c == EC - 1))
            last.then_inc(modc_full, 1)
            for k, blk in enumerate((2, 5)):
                for c in range(EC):
                    last = mm(PB[0:B, k * E:(k + 1) * E], sT[:, c, :], mod_sb[:, c, blk * E:(blk + 1) * E],
                              start=(c == 0), stop=(c == EC - 1))
            last.then_inc(gate_full, 1)
            pe.wait_ge(modc_ready, 2)
            pe.wait_ge(gate_step, 1)
            pe.wait_ge(weights_loaded, 16 * 8)
            pe.wait_ge(const_ready, 1)
            pe.wait_ge(bf_ready, 1)

            def xn_transpose(b, c):
                if c == 0:
                    pe.wait_ge(xn1_ready, b + 1)
                    if later(SL * b - 1):
                        pe.wait_ge(m2_ready, SL * b - 1)
                else:
                    pe.wait_ge(hT_done, EC * b + c)
                for t in range(TT):
                    last = nc.tensor.transpose(PA[:, t * P:(t + 1) * P], xin[:, t, c * P:(c + 1) * P], ident[:, :])
                last.then_inc(xnT_full, 1)

            def project_piece(b, i, which, j):
                n = SL * b + i
                full, piece, sp_tile = (q_full, q_piece, qsp) if which == 0 else (k_full, k_piece, ksp)
                if j == 0:
                    if which == 1:
                        pe.wait_ge(q_piece, NPC * (n + 1))
                    elif i == 0:
                        pe.wait_ge(hT_done, EC * (b + 1))
                    else:
                        if later(n):
                            pe.wait_ge(v_done, n)
                        if later(n - 1):
                            pe.wait_ge(m2_ready, n - 1)
                    for c in range(EC):
                        last = mm(PA[:, :], qk_sb[:, c, which * E + i * P:which * E + (i + 1) * P], hT[:, c, :],
                                  start=(c == 0), stop=(c == EC - 1))
                else:
                    pe.wait_ge(piece, NPC * n + j)
                    last = mm(PA[:, :], nidentb[:, :], sp_tile[:, j - 1, :], start=False, stop=True,
                              skip_group_check=True)
                last.then_inc(full, 1)

            def project_v(n, i):
                pe.wait_ge(k_piece, NPC * (n + 1))
                for t in range(TT):
                    for c in range(EC):
                        last = mm(PA[:, t * P:(t + 1) * P], hT[:, c, t * P:(t + 1) * P],
                                  v_sb[:, c, i * P:(i + 1) * P], start=(c == 0), stop=(c == EC - 1))
                last.then_inc(v_full, 1)

            def max_unit(n, r, u):
                if u == 0:
                    pe.wait_ge(stack_loaded, 16 * (len(QR) + len(KR)) * (n + 1))
                if later(GS * UM * n + u - 1):
                    pe.wait_ge(max_read, GS * UM * n + u - 1)
                bankt = MX[u % 2]
                h0, nh, qb = max_parts(u)
                w = (qb + 1) * P
                for k in range(nh):
                    mm(bankt[:, k * w:(k + 1) * w], Qs[r][0:KQ, h0 + k, qb * P:(qb + 1) * P],
                       Ks[r][0:KQ, h0 + k, 0:w], start=(k == 0), stop=False, skip_group_check=True)
                for k in range(nh):
                    last = mm(bankt[:, (k + 1) * w - P:(k + 1) * w], identb[:, :], maskb[:, :],
                              start=False, stop=(k == nh - 1), skip_group_check=True)
                last.then_inc(max_full, 1)

            def max_transpose(n):
                pe.wait_ge(max_read, GS * UM * (n + 1))
                pe.wait_ge(v_done, min(n + 2, SL * B) if isinstance(n, int) else n + 2)
                for qb in range(TT):
                    last = nc.tensor.transpose(PA[0:HS, qb * P:(qb + 1) * P], rmax[:, qb, :], ident[:, :])
                last.then_inc(mT_full, 1)

            def score_unit(n, r, u):
                if u == 0:
                    pe.wait_ge(m_loaded, 16 * (n + 1))
                if later(GS * UE * n + u - 1):
                    pe.wait_ge(exp_done, GS * UE * n + u - 1)
                at = 0
                for h, kb in score_parts(u):
                    w = T - kb * P
                    last = mm(ES[u % 2][:, at:at + w], Ks[r][:, h, kb * P:(kb + 1) * P], Qs[r][:, h, kb * P:T],
                              start=True, stop=True)
                    at += w
                last.then_inc(sc_full, 1)

            def pv(n, r, g):
                pe.wait_ge(v_done, n + 1)
                if later(GS * n + g - 1):
                    pe.wait_ge(oT_done, GS * n + g - 1)
                for kb in range(TT):
                    pe.wait_ge(masked, TT * (GS * n + g) + kb + 1)
                    w = T - kb * P
                    for h in range(HG):
                        last = mm(OT[g][CT * h:CT * (h + 1), kb * P:T], Va[r][:, kb, HG * g + h, :],
                                  PT[g][:, h, KBO[kb]:KBO[kb] + w], start=(kb == 0), stop=(kb == TT - 1))
                last.then_inc(pv_full, 1)

            def head_transpose(b, t):
                if t == 0:
                    pe.wait_ge(oT_done, SL * GS * (b + 1))
                    if later(2 * b):
                        pe.wait_ge(y_done, 2 * b)
                else:
                    pe.wait_ge(attn_done, TT * b + t)
                for g in range(SL * GS):
                    last = nc.tensor.transpose(PB[:, g * P:(g + 1) * P], oT[:, g, t * P:(t + 1) * P], ident[:, :])
                last.then_inc(oTT_full, 1)

            def attn_transpose(b, c):
                if c == 0:
                    pe.wait_ge(attn_done, TT * (b + 1))
                else:
                    pe.wait_ge(aT_done, EC * b + c)
                for t in range(TT):
                    last = nc.tensor.transpose(PB[:, t * P:(t + 1) * P], attn[:, t, c * P:(c + 1) * P], ident[:, :])
                last.then_inc(aT_full, 1)

            def token_product(actT, w, j):
                for t in (2 * j, 2 * j + 1):
                    for c in range(EC):
                        last = mm(PB[:, (t % 2) * E:(t % 2 + 1) * E], actT[:, c, t * P:(t + 1) * P], w[:, c, :],
                                  start=(c == 0), stop=(c == EC - 1))
                return last

            def out_project(b, j):
                if j == 0:
                    pe.wait_ge(aT_done, EC * (b + 1))
                    pe.wait_ge(gates_folded, 2 * b + 1)
                else:
                    pe.wait_ge(x1_done, 2 * b + j)
                token_product(aT, og_sb, j).then_inc(o_full, 1)

            def xn2_transpose(b, c):
                if c == 0:
                    pe.wait_ge(xn2_ready, b + 1)
                else:
                    pe.wait_ge(h2_done, EC * b + c)
                for t in range(TT):
                    last = nc.tensor.transpose(PB[:, t * P:(t + 1) * P], attn[:, t, c * P:(c + 1) * P], ident[:, :])
                last.then_inc(xn2T_full, 1)

            def key_project(b, co):
                if co == 0:
                    pe.wait_ge(mixed, 2 * b + 1)
                else:
                    pe.wait_ge(relu_done, EC * b + co)
                for c in range(EC):
                    last = mm(PB[:, :], k_sb[:, c, co * P:(co + 1) * P], xk[:, c, :],
                              start=(c == 0), stop=(c == EC - 1))
                last.then_inc(kp_full, 1)

            def receptance_project(b, j):
                if j == 0:
                    pe.wait_ge(mixed, 2 * b + 2)
                    pe.wait_ge(relu_done, EC * (b + 1))
                else:
                    pe.wait_ge(tanh_done, 2 * b + j)
                token_product(xr, r_sb, j).then_inc(rp_full, 1)

            def value_project(b, j):
                if j == 0:
                    pe.wait_ge(tanh_done, 2 * (b + 1))
                    pe.wait_ge(act_done, EC * (b + 1))
                    pe.wait_ge(gates_folded, 2 * b + 2)
                else:
                    pe.wait_ge(y_done, 2 * b + j)
                token_product(ka, cg_sb, j).then_inc(vp_full, 1)

            def pre_step(b, i, k):
                k0 = 6 if i == 0 else 2
                if i == 0 and k in (4, 5):
                    xn_transpose(b, k - 4)
                if k0 <= k < k0 + 3:
                    project_piece(b, i, 0, k - k0)
                elif k0 + 3 <= k < k0 + 6:
                    project_piece(b, i, 1, k - k0 - 3)
                elif k == k0 + 6:
                    project_v(SL * b + i, i)

            def post_step(b, i, k):
                if i == 0:
                    if k in (3, 5, 7, 9):
                        head_transpose(b, (k - 3) // 2)
                    elif k in (11, 13):
                        attn_transpose(b, (k - 11) // 2)
                    elif k in (15, 16):
                        out_project(b, k - 15)
                    elif k in (20, 21):
                        xn2_transpose(b, k - 20)
                else:
                    if k in (4, 6):
                        key_project(b, (k - 4) // 2)
                    elif k in (9, 11):
                        receptance_project(b, (k - 9) // 2)
                    elif k in (13, 15):
                        value_project(b, (k - 13) // 2)

            def prologue():
                for i in range(SL):
                    for k in range(22):
                        pre_step(0, i, k)
                for u in range(GS * UM):
                    max_unit(0, 0, u)
                max_transpose(0)

            def half(b, par, i, first, last):
                n = SL * b + i
                r, rn = ring(par, i), ring(par, 1) if i == 0 else ring(1 - par, 0)
                for k in range(GS * UM):
                    g, u = divmod(k, UM)
                    if k < UM and (i == 0 or not last):
                        max_unit(n + 1, rn, 2 * k)
                        max_unit(n + 1, rn, 2 * k + 1)
                    if u < UE:
                        score_unit(n, r, UE * g + u)
                    if k == 2 and not (first and i == 0):
                        pv(n - 1, (r - 1) % RING, 1)
                    if k == 14:
                        pv(n, r, 0)
                    if not last:
                        pre_step(b + 1, i, k)
                    if k == 13 and (i == 0 or not last):
                        max_transpose(n + 1)
                    if not first:
                        post_step(b - 1, i, k)

            def epilogue():
                pv(SL * B - 1, RING - 1, 1)
                for i in range(SL):
                    for k in range(22):
                        post_step(B - 1, i, k)

            slots(pe, prologue, half, epilogue)

        @block.scalar
        def _(act):
            fn = nc.scalar.activation
            act.wait_ge(cond_loaded, 32)
            fn(th_sb, cond_sb, ACT.Tanh, scale=0.5).then_inc(th_ready, 1)

            def norm1(b):
                act.wait_ge(rstd1_ready, b + 1)
                for t in range(TT):
                    last = fn(xin[:, t, :], xin[:, t, :], ACT.Identity, bias=nm1[:, t:t + 1], scale=rs1[:, t:t + 1])
                last.then_inc(xn1_ready, 1)

            def modulate1(b, c):
                act.wait_ge(xnT_full, EC * b + c + 1)
                act.wait_ge(mpre_loaded, 16 * (b + 1))
                if c == 0:
                    if later(SL * b):
                        act.wait_ge(v_full, SL * b)
                fn(hT[:, c, :], PA[:, :], ACT.Identity, bias=mpre[:, c:c + 1], scale=mpre[:, EC + c:EC + c + 1])\
                    .then_inc(hT_done, 1)

            def piece(n, which, j):
                full, done, tile, stored = ((q_full, q_piece, qsp, q_stored) if which == 0 else
                                            (k_full, k_piece, ksp, k_stored))
                act.wait_ge(full, NPC * n + j + 1)
                if j == 0:
                    if later(16 * n):
                        act.wait_ge(stored, 16 * n)
                fn(tile[:, j, :], PA[:, :], ACT.Copy).then_inc(done, 1)

            def max_piece(n):
                act.wait_ge(mT_full, n + 1)
                if later(16 * n):
                    act.wait_ge(m_stored, 16 * n)
                fn(mT[:, 0, :], PA[0:HS, :], ACT.Copy, scale=-1.0).then_inc(m1_ready, 1)

            def exp_unit(n, u):
                g, v = divmod(u, UE)
                act.wait_ge(sc_full, GS * UE * n + u + 1)
                if v == 0:
                    if later(GS * n + g - 1):
                        act.wait_ge(pv_full, GS * n + g - 1)
                pair, w = divmod(v, 5)
                if w < 4:
                    h, part = 2 * pair + w // 2, w % 2
                    fn(PT[g][:, h, part * T:(part + 1) * T], ES[u % 2][:, :], ACT.Exp, scale=SCALE)\
                        .then_inc(exp_done, 1)
                else:
                    fn(PT[g][:, 2 * pair:2 * pair + 2, 2 * T:HT], ES[u % 2][:, :].rearrange("p (h q) -> p h q", h=2),
                       ACT.Exp, scale=SCALE).then_inc(exp_done, 1)

            def take_pv(n, b, i, g):
                act.wait_ge(pv_full, GS * n + g + 1)
                if later(TT * b):
                    act.wait_ge(oTT_full, TT * b)
                fn(oT[:, GS * i + g, :], OT[g][:, :], ACT.Copy).then_inc(oT_done, 1)

            def take_attn(b, c):
                act.wait_ge(aT_full, EC * b + c + 1)
                fn(aT[:, c, :], PB[:, :], ACT.Copy).then_inc(aT_done, 1)

            def norm2(b):
                act.wait_ge(rstd2_ready, b + 1)
                for t in range(TT):
                    last = fn(attn[:, t, :], x1[:, t, :], ACT.Identity, bias=nm2[:, t:t + 1], scale=rs2[:, t:t + 1])
                last.then_inc(xn2_ready, 1)

            def modulate2(b, c):
                act.wait_ge(xn2T_full, EC * b + c + 1)
                if later(2 * b):
                    act.wait_ge(mixed, 2 * b)
                fn(h2[:, c, 1:T + 1], PB[:, :], ACT.Identity, bias=mpost[:, 4 + c:5 + c],
                   scale=mpost[:, 6 + c:7 + c]).then_inc(h2_done, 1)

            def relu(b, c):
                act.wait_ge(kp_full, EC * b + c + 1)
                if later(2 * b):
                    act.wait_ge(vp_full, 2 * b)
                fn(ka[:, c, :], PB[:, :], ACT.Relu).then_inc(relu_done, 1)

            def receptance(b, j):
                act.wait_ge(rp_full, 2 * b + j + 1)
                if later(16 * b):
                    act.wait_ge(out_stored, 16 * b)
                fn(y[:, 2 * j:2 * j + 2, :], PB[:, :].rearrange("p (t e) -> p t e", t=2), ACT.Tanh, scale=0.5)\
                    .then_inc(tanh_done, 1)

            def pre_step(b, i, k):
                k0 = 6 if i == 0 else 2
                if i == 0 and k == 2:
                    norm1(b)
                if i == 0 and k in (4, 5):
                    modulate1(b, k - 4)
                if k in (k0, k0 + 2):
                    piece(SL * b + i, 0, k - k0)
                elif k in (k0 + 3, k0 + 5):
                    piece(SL * b + i, 1, k - k0 - 3)

            def post_step(b, i, k):
                if i == 0:
                    if k in (11, 13):
                        take_attn(b, (k - 11) // 2)
                    elif k == 18:
                        norm2(b)
                    elif k in (20, 21):
                        modulate2(b, k - 20)
                else:
                    if k in (4, 6):
                        relu(b, (k - 4) // 2)
                    elif k in (9, 11):
                        receptance(b, (k - 9) // 2)

            def prologue():
                for i in range(SL):
                    for k in range(22):
                        pre_step(0, i, k)
                max_piece(0)

            def half(b, par, i, first, last):
                n = SL * b + i
                for k in range(GS * UM):
                    g, u = divmod(k, UM)
                    if u < UE:
                        exp_unit(n, UE * g + u)
                    if k == 2 and not (first and i == 0):
                        if i == 0:
                            take_pv(n - 1, b - 1, 1, 1)
                        else:
                            take_pv(n - 1, b, 0, 1)
                    if k == 14:
                        take_pv(n, b, i, 0)
                    if not last:
                        pre_step(b + 1, i, k)
                    if k == 13 and (i == 0 or not last):
                        max_piece(n + 1)
                    if not first:
                        post_step(b - 1, i, k)

            def epilogue():
                take_pv(SL * B - 1, B - 1, 1, 1)
                for i in range(SL):
                    for k in range(22):
                        post_step(B - 1, i, k)

            slots(act, prologue, half, epilogue)

        @block.vector
        def _(dve):
            v = nc.vector
            v.memset(h2[:, :, 0:1], 0.0)
            for r in range(RING):
                v.memset(Va[r][:, :, :, D:CT], 1.0)
            for r in range(RING):
                last = v.memset(Ks[r][KQ:KS, :, :], 1.0)
            last.then_inc(bf_ready, 1)
            dve.wait_ge(th_ready, 1)
            v.scalar_tensor_tensor(out=sT, in0=th_sb, scalar=1.0, in1=cond_sb, op0=ALU.add, op1=ALU.mult)\
                .then_inc(silu_ready, 1)
            dve.wait_ge(modc_full, 1)
            for k in range(4):
                src = PA[:, EC * k * B:EC * (k + 1) * B].rearrange("p (c b) -> p b c", c=EC)
                last = v.tensor_scalar(modc[:, :, EC * k:EC * (k + 1)], src, 0.5, float(k % 2), ALU.mult, ALU.add)
                if k >= 2:
                    last.then_inc(modc_ready, 1)
            dve.wait_ge(gate_full, 1)
            v.tensor_scalar(gr[0], PB[0:B, :], 0.5, None, ALU.mult).then_inc(gate_step, 1)
            dve.wait_ge(gate_step, 1)
            v.tensor_scalar(gr[1], gr[0], -1.0, None, ALU.mult).then_inc(gate_step, 1)
            dve.wait_ge(gate_step, 2)
            v.scalar_tensor_tensor(out=gr[2], in0=gr[0], scalar=0.25, in1=gr[1], op0=ALU.max, op1=ALU.max)\
                .then_inc(gate_step, 1)
            dve.wait_ge(gate_step, 3)
            v.tensor_scalar(gr[1], gr[0], 0.0, 2.0, ALU.is_ge, ALU.mult).then_inc(gate_step, 1)
            dve.wait_ge(gate_step, 4)
            v.scalar_tensor_tensor(out=gr[3], in0=gr[1], scalar=-1.0, in1=gr[2], op0=ALU.add, op1=ALU.mult)\
                .then_inc(gate_step, 1)
            dve.wait_ge(gate_step, 5)
            v.tensor_scalar(gr[3][:, E:2 * E], gr[3][:, E:2 * E], 0.5, None, ALU.mult).then_inc(gate_ready, 1)

            def stats(b, src, st, mv, rs, nm, step, ready):
                done = [STATS_STEPS * b]

                def link(ins):
                    ins.then_inc(step, 1)
                    done[0] = done[0] + 1
                    dve.wait_ge(step, done[0])

                for t in range(TT):
                    last = v.bn_stats(st[:, t, :], src[:, t, :])
                link(last)
                v.memset(nwt[:, 3, :], 0.0)
                for t in range(TT):
                    last = v.bn_aggr(mv[:, t, :], st[:, t, :])
                link(last)
                ve, nv, yy, t2 = (nwt[:, k, :] for k in range(4))
                link(v.tensor_scalar(ve, mv[:, :, 1], EPS, None, ALU.add))
                v.tensor_scalar(nv, ve, -0.5, None, ALU.mult)
                link(v.tensor_scalar(rs[:, :].bitcast(i32), ve.bitcast(i32), -0.5, RSQRT_SEED, ALU.mult, ALU.add))
                for _ in range(NEWTON):
                    link(v.tensor_tensor(yy, rs[:, :], rs[:, :], ALU.mult))
                    link(v.tensor_tensor(t2, yy, nv, ALU.mult))
                    link(v.scalar_tensor_tensor(out=rs[:, :], in0=t2, scalar=1.5, in1=rs[:, :], op0=ALU.add,
                                                op1=ALU.mult))
                v.scalar_tensor_tensor(out=nm[:, :], in0=mv[:, :, 0], scalar=-1.0, in1=rs[:, :], op0=ALU.mult,
                                       op1=ALU.mult).then_inc(ready, 1)

            def stats1(b):
                dve.wait_ge(x_loaded, 16 * (b + 1))
                if later(b):
                    dve.wait_ge(xn1_ready, b)
                stats(b, xin, st1, mv1, rs1, nm1, stats1_step, rstd1_ready)

            def piece(n, which, j):
                full, done, tile = (q_full, q_piece, qsp) if which == 0 else (k_full, k_piece, ksp)
                dve.wait_ge(full, NPC * n + j + 1)
                v.tensor_copy(tile[:, j, :], PA[:, :]).then_inc(done, 1)

            def take_v(n, r):
                dve.wait_ge(v_full, n + 1)
                if later(GS * (n - RING + 1)):
                    dve.wait_ge(pv_full, GS * (n - RING + 1))
                v.tensor_copy(Va[r][:, :, :, 0:D], PA[:, :].rearrange("p (t h d) -> p t h d", t=TT, h=HS))\
                    .then_inc(v_done, 1)

            def max_unit(n, u):
                dve.wait_ge(max_full, GS * UM * n + u + 1)
                if u == 0:
                    if later(n):
                        dve.wait_ge(mT_full, n)
                h0, nh, qb = max_parts(u)
                w = (qb + 1) * P
                v.reduce_max(rmax[:, qb, h0:h0 + nh], MX[u % 2][:, 0:nh * w].rearrange("p (h k) -> p h k", h=nh),
                             axis=AX.X).then_inc(max_read, 1)

            def max_piece(n):
                dve.wait_ge(m1_ready, n + 1)
                dve.wait_ge(mT_full, n + 1)
                v.scalar_tensor_tensor(out=mT[:, 1, :], in0=PA[0:HS, :], scalar=-1.0, in1=mT[:, 0, :], op0=ALU.mult,
                                       op1=ALU.subtract).then_inc(m2_ready, 1)

            def normalise(b, t):
                dve.wait_ge(oTT_full, TT * b + t + 1)
                heads = PB[:, :].rearrange("p (h c) -> p h c", c=CT)
                v.reciprocal(rec[:, :], heads[:, :, D]).then_inc(rec_ready, 1)
                dve.wait_ge(rec_ready, TT * b + t + 1)
                if t == 0:
                    if later(EC * b):
                        dve.wait_ge(xn2T_full, EC * b)
                v.tensor_tensor(attn[:, t, :].rearrange("p (h d) -> p h d", d=D), heads[:, :, 0:D],
                                rec[:, :].unsqueeze(2).to_broadcast([P, H, D]), ALU.mult).then_inc(attn_done, 1)

            def add_attention(b, j):
                dve.wait_ge(o_full, 2 * b + j + 1)
                dve.wait_ge(post_loaded, 48 * (b + 1))
                v.tensor_tensor(x1[:, 2 * j:2 * j + 2, :], PB[:, :].rearrange("p (t e) -> p t e", t=2),
                                x1[:, 2 * j:2 * j + 2, :], ALU.add).then_inc(x1_done, 1)

            def stats2(b):
                dve.wait_ge(x1_done, 2 * (b + 1))
                if later(b):
                    dve.wait_ge(xn2_ready, b)
                stats(b, x1, st2, mv2, rs2, nm2, stats2_step, rstd2_ready)

            def mix(b, which, dst):
                dve.wait_ge(diff_done, b + 1)
                dve.wait_ge(rp_full, 2 * b)
                for c in range(EC):
                    last = v.scalar_tensor_tensor(out=dst[:, c, :], in0=aT[:, c, :], scalar=mu_sb[:, which, c:c + 1],
                                                  in1=h2[:, c, 0:T], op0=ALU.mult, op1=ALU.add)
                last.then_inc(mixed, 1)

            def gate_value(b, j):
                dve.wait_ge(vp_full, 2 * b + j + 1)
                dve.wait_ge(tanh_done, 2 * b + j + 1)
                yj = y[:, 2 * j:2 * j + 2, :]
                v.scalar_tensor_tensor(out=yj, in0=yj, scalar=1.0, in1=PB[:, :].rearrange("p (t e) -> p t e", t=2),
                                       op0=ALU.add, op1=ALU.mult).then_inc(y_done, 1)

            def pre_step(b, i, k, r):
                k0 = 6 if i == 0 else 2
                n = SL * b + i
                if i == 0 and k == 1:
                    stats1(b)
                if k == k0 + 1:
                    piece(n, 0, 1)
                elif k == k0 + 4:
                    piece(n, 1, 1)
                elif k == k0 + 6:
                    take_v(n, r)

            def post_step(b, i, k):
                if i == 0:
                    if k in (3, 5, 7, 9):
                        normalise(b, (k - 3) // 2)
                    elif k in (15, 16):
                        add_attention(b, k - 15)
                        if k == 16:
                            stats2(b)
                else:
                    if k == 1:
                        mix(b, 1, xk)
                    elif k == 2:
                        mix(b, 0, xr)
                    elif k in (13, 15):
                        gate_value(b, (k - 13) // 2)

            dve.wait_ge(weights_loaded, 16 * 8)

            def prologue():
                for i in range(SL):
                    for k in range(22):
                        pre_step(0, i, k, i)
                for u in range(GS * UM):
                    max_unit(0, u)
                max_piece(0)

            def half(b, par, i, first, last):
                n = SL * b + i
                for k in range(GS * UM):
                    if k < UM and (i == 0 or not last):
                        max_unit(n + 1, 2 * k)
                        max_unit(n + 1, 2 * k + 1)
                    if not last:
                        pre_step(b + 1, i, k, ring(1 - par, i))
                    if k == 13 and (i == 0 or not last):
                        max_piece(n + 1)
                    if not first:
                        post_step(b - 1, i, k)

            def epilogue():
                for i in range(SL):
                    for k in range(22):
                        post_step(B - 1, i, k)

            slots(dve, prologue, half, epilogue)

        @block.gpsimd
        def _(pool):
            g_ = nc.gpsimd
            g_.memset(ident[:, :], 0.0)
            g_.memset(pool_mark[:, :], 0.0)
            g_.memset(maskb[:, :], 0.0).then_inc(zeros_ready, 1)
            pool.wait_ge(zeros_ready, 1)
            g_.affine_select(out=ident[:, :], in_=ident[:, :], compare_op=ALU.not_equal, fill=1.0, base=0,
                             pattern=[[-1, P]], channel_multiplier=1).then_inc(ident_ready, 1)
            g_.affine_select(out=maskb[:, :], in_=maskb[:, :], compare_op=ALU.is_ge, fill=NEG, base=0,
                             pattern=[[-1, P]], channel_multiplier=1)
            pool.wait_ge(ident_ready, 1)
            g_.tensor_copy(identb[:, :], ident[:, :])
            g_.tensor_scalar(nidentb[:, :], ident[:, :], -1.0, None, ALU.mult).then_inc(const_ready, 1)
            pool.wait_ge(weights_loaded, 16 * 8)

            def mask(n, g):
                pool.wait_ge(exp_done, UE * (GS * n + g + 1))
                g_.tensor_tensor(pool_mark[:, :], pool_mark[:, :], pool_mark[:, :], ALU.mult)
                for kb in range(TT):
                    blk = PT[g][:, :, KBO[kb]:KBO[kb] + P]
                    g_.affine_select(out=blk, in_=blk, compare_op=ALU.is_ge, fill=0.0, base=0,
                                     pattern=[[0, HG], [1, P]], channel_multiplier=-1).then_inc(masked, 1)

            def fold_gates(b):
                pool.wait_ge(post_loaded, 48 * (b + 1))
                if later(2 * b):
                    pool.wait_ge(o_full, 2 * b)
                ga = gate_sb[:, 0:E].unsqueeze(1).to_broadcast([P, EC, E])
                gb = gate_sb[:, E:2 * E].unsqueeze(1).to_broadcast([P, EC, E])
                g_.tensor_tensor(og_sb[:, :, :], o_sb[:, :, :], ga, ALU.mult).then_inc(gates_folded, 1)
                if later(2 * b):
                    pool.wait_ge(vp_full, 2 * b)
                g_.tensor_tensor(cg_sb[:, :, :], c_sb[:, :, :], gb, ALU.mult).then_inc(gates_folded, 1)

            def diff(b):
                pool.wait_ge(h2_done, EC * (b + 1))
                pool.wait_ge(o_full, 2 * (b + 1))
                g_.tensor_tensor(aT[:, :, :], h2[:, :, 1:T + 1], h2[:, :, 0:T], ALU.subtract)\
                    .then_inc(diff_done, 1)

            def square(b, c):
                pool.wait_ge(relu_done, EC * b + c + 1)
                g_.tensor_tensor(ka[:, c, :], ka[:, c, :], ka[:, c, :], ALU.mult).then_inc(act_done, 1)

            def finish(b):
                pool.wait_ge(y_done, 2 * (b + 1))
                g_.tensor_tensor(y[:, :, :], y[:, :, :], x1[:, :, :], ALU.add).then_inc(out_added, 1)
                pool.wait_ge(out_added, b + 1)
                pool.dma_start(out[b].rearrange("(t p) e -> p t e", p=P), y[:, :, :]).then_inc(out_stored, 16)

            def post_step(b, i, k):
                if i == 0:
                    if k == 4:
                        fold_gates(b)
                else:
                    if k == 0:
                        diff(b)
                    elif k in (4, 6):
                        square(b, (k - 4) // 2)
                    elif k == 15:
                        finish(b)

            def prologue():
                pass

            def half(b, par, i, first, last):
                n = SL * b + i
                for k in range(GS * UM):
                    if k == 10:
                        mask(n, 0)
                    if not first:
                        post_step(b - 1, i, k)
                    if k == 21:
                        mask(n, 1)

            def epilogue():
                for i in range(SL):
                    for k in range(22):
                        post_step(B - 1, i, k)

            slots(pool, prologue, half, epilogue)


def sb_view(tile, P, a, n):
    flat = tile[:, :, :].rearrange("p a b -> p (a b)")
    return flat[:, 0:a * n].rearrange("p (a n) -> p a n", a=a)


def bcast_rows(dram, b, P):
    return dram[b].unsqueeze(0).to_broadcast([P, dram.shape[1]])


def max_parts(u):
    g, v = divmod(u, 11)
    if v < 8:
        return 4 * g + v // 2, 1, 3 - v % 2
    if v < 10:
        return 4 * g + 2 * (v - 8), 2, 1
    return 4 * g, 4, 0


def score_parts(u):
    pair, w = divmod(u, 5)
    if w < 4:
        h = 2 * pair + w // 2
        return [(h, 0)] if w % 2 == 0 else [(h, 1), (h, 3)]
    return [(2 * pair, 2), (2 * pair + 1, 2)]


def kernel(**inputs):
    import numpy as _np
    import concourse.bacc as _bacc
    from concourse import mybir as _mybir
    from concourse.bass_utils import run_bass_kernel_spmd as _run

    a = {k: _np.asarray(v) for k, v in inputs.items()}
    E, D, H = 256, 16, 16
    in_w = a["L0_attn_in_proj_weight"].T
    qk = in_w[:, 0:2 * E].reshape(E, 2, 2, H // 2, D).transpose(0, 1, 2, 4, 3).reshape(E, 2 * E)
    arrays = {
        "x": a["L0_attn_query"], "qk_w": qk, "v_w": in_w[:, 2 * E:3 * E], "o_w": a["L0_attn_out_proj_weight"].T,
        "r_w": a["L0_ffn_W_r"].T, "k_w": a["L0_ffn_W_k"].T, "c_w": a["L0_ffn_W_v"].T,
        "mu_r": a["L0_ffn_mu_r"].reshape(2, 128).T, "mu_k": a["L0_ffn_mu_k"].reshape(2, 128).T,
        "cond": a["L0_c"].T, "mod_w": a["L0_wmod"],
    }
    arrays = {k: _np.ascontiguousarray(v) for k, v in arrays.items()}
    nc = _bacc.Bacc("TRN2", target_bir_lowering=False, num_devices=1)
    args = [nc.dram_tensor(k, v.shape, _mybir.dt.from_np(v.dtype), kind="ExternalInput").ap()
            for k, v in arrays.items()]
    out = nc.dram_tensor("out", a["L0_attn_query"].shape, _mybir.dt.float32, kind="ExternalOutput").ap()
    adaln_attention_channel_mix_kernel(nc, *args, out)
    r = _run(nc, [arrays], core_ids=[0])
    return r.results[0]["out"]
```

```python
import concourse.bass as bass
from concourse import mybir
from contextlib import ExitStack


def adaln_attention_channel_mix_kernel(nc, x, qk_w, v_w, o_w, r_w, k_w, c_w, mu_r, mu_k, cond, mod_w, out):
    f32, bf16, i32 = mybir.dt.float32, mybir.dt.bfloat16, mybir.dt.int32
    ALU, ACT, AX = mybir.AluOpType, mybir.ActivationFunctionType, mybir.AxisListType

    B, T, E = x.shape
    P = 128
    TT = T // P
    EC = E // P
    H, D = 16, 16
    HS = P // D
    SL = H // HS
    HG = 4
    GS = HS // HG
    CT = 32
    NPC = 3
    KQ = 6 * D
    KS = KQ + 2
    RING = 4
    HT = sum(T - kb * P for kb in range(TT))
    SCALE = 1.0 / D ** 0.5
    EPS = 1e-5
    RSQRT_SEED = float(0x5f3759df)
    NEWTON = 3
    NEWTON_STEPS = 4 * NEWTON + 1
    NEG = -1e30
    UM = 11
    UE = 10
    KBO = [0, T, 2 * T, T + 384]
    QR, KR = [(0, 3, 0), (3, 2, 0), (5, 1, 0)], [(0, 0), (1, 0), (2, 0), (3, 1), (4, 1), (5, 2)]

    NPOS = GS * UM
    PV_BEFORE = 2
    PV_THIS = 13
    MAX_STARTS = 0
    MAX_ENDS = 16
    MAXT_AT = (17, 17)
    NORM1_AT = 0
    XNT_AT = (2, 4)
    Q_AT = ((5, 7, 9), (2, 4, 6))
    K_AT = ((11, 12, 13), (8, 10, 13))
    V_AT = (15, 16)
    STATS1_AT = (14, 15, 18, 19)
    FOLD_AT = 4
    HEADT_AT = (3, 5, 7, 10)
    ATTNT_AT = (11, 12)
    OUT_AT = (14, 16)
    STATS2_AT = (17, 18, 19, 21)
    NORM2_AT = 25
    XN2T_AT = (27, 29)
    DIFF_AT = 30
    MIX_AT = (31, 32)
    KEY_AT = (33, 35)
    REC_AT = (38, 39)
    VAL_AT = (41, 43)
    MASK_AT = (10, 21)
    SCORE_FIRST = True
    def max_units(k):
        span = MAX_ENDS - MAX_STARTS
        return range(*(max(0, min(NPOS, NPOS * (j - MAX_STARTS) // span)) for j in (k, k + 1)))

    gate_dram = nc.dram_tensor("gate_rows", [B, 2 * E], f32, kind="Internal").ap()
    modc_dram = nc.dram_tensor("mod_columns", [B, P, 8], f32, kind="Internal").ap()
    q_dram = nc.dram_tensor("q_pieces", [RING, NPC, P, T], bf16, kind="Internal").ap()
    k_dram = nc.dram_tensor("k_pieces", [RING, NPC, P, T], bf16, kind="Internal").ap()
    m_dram = nc.dram_tensor("max_pieces", [RING, 2, HS, T], bf16, kind="Internal").ap()

    ctx = ExitStack()
    with ctx:
        def sb(name, shape, dt=f32):
            return ctx.enter_context(nc.sbuf_tensor(name, shape, dt))

        def sem(name):
            return ctx.enter_context(nc.semaphore(name))

        qk_sb = sb("qk_sb", [P, EC, 2 * E])
        v_sb = sb("v_sb", [P, EC, E])
        o_sb = sb("o_sb", [P, EC, E])
        r_sb = sb("r_sb", [P, EC, E])
        k_sb = sb("k_sb", [P, EC, E])
        c_sb = sb("c_sb", [P, EC, E])
        og_sb = sb("og_sb", [P, EC, E])
        cg_sb = sb("cg_sb", [P, EC, E])
        mu_sb = sb("mu_sb", [P, 2, EC])
        gate_sb = sb("gate_sb", [P, 2 * E])
        mpre = sb("mpre", [P, 8])
        mpost = sb("mpost", [P, 8])
        ident = sb("ident", [P, P])
        identb = sb("identb", [P, P], bf16)
        nidentb = sb("nidentb", [P, P], bf16)
        maskb = sb("maskb", [P, P], bf16)
        xin = sb("xin", [P, TT, E])
        st1 = sb("st1", [P, TT, 6])
        mv1 = sb("mv1", [P, TT, 2])
        nw1 = sb("nw1", [P, 4, TT])
        rs1 = sb("rs1", [P, TT])
        nm1 = sb("nm1", [P, TT])
        hT = sb("hT", [P, EC, T])
        qsp = sb("qsp", [P, NPC, T], bf16)
        ksp = sb("ksp", [P, NPC, T], bf16)
        Qs = [sb(f"Qs{r}", [KS, HS, T], bf16) for r in range(RING)]
        Ks = [sb(f"Ks{r}", [KS, HS, T], bf16) for r in range(RING)]
        Va = [sb(f"Va{r}", [P, TT, HS, CT]) for r in range(RING)]
        rmax = sb("rmax", [P, TT, HS])
        mT = sb("mT", [HS, 2, T], bf16)
        PT = [sb(f"PT{g}", [P, HG, HT]) for g in range(GS)]
        oT = sb("oT", [P, SL * GS, T])
        pool_mark = sb("pool_mark", [P, 1])
        newton_c = sb("newton_c", [P, 2, TT])
        rec = sb("rec", [P, TT, H])
        attn = sb("attn", [P, TT, E])
        aT = sb("aT", [P, EC, T])
        x1 = sb("x1", [P, TT, E])
        st2 = sb("st2", [P, TT, 6])
        mv2 = sb("mv2", [P, TT, 2])
        nw2 = sb("nw2", [P, 4, TT])
        rs2 = sb("rs2", [P, TT])
        nm2 = sb("nm2", [P, TT])
        h2 = sb("h2", [P, EC, T + 1])
        xr = sb("xr", [P, EC, T])
        xk = sb("xk", [P, EC, T])
        ka = sb("ka", [P, EC, T])
        y = sb("y", [P, TT, E])
        mod_sb = sb_view(PT[0], P, EC, 6 * E)
        cond_sb = y[:, 0, 0:EC * B].rearrange("p (c b) -> p c b", c=EC)
        th_sb = y[:, 1, 0:EC * B].rearrange("p (c b) -> p c b", c=EC)
        sT = y[:, 2, 0:EC * B].rearrange("p (c b) -> p c b", c=EC)
        gr = [xr[0:B, 0, :], xr[0:B, 1, :], xk[0:B, 0, :], xk[0:B, 1, :]]
        modc = ka[:, 0, 0:B * 8].rearrange("p (b k) -> p b k", k=8)

        def bank(name):
            return ctx.enter_context(nc.psum_tensor(name, [P, 512], f32))

        ES = [bank(f"scores{i}") for i in range(2)]
        MX = [bank(f"maxed{i}") for i in range(2)]
        OT = [bank(f"pv{i}") for i in range(2)]
        PA = bank("pre_bank")
        PB = bank("post_bank")

        weights_loaded = sem("weights_loaded")
        cond_loaded = sem("cond_loaded")
        modw_loaded = sem("modw_loaded")
        zeros_ready = sem("zeros_ready")
        ident_ready = sem("ident_ready")
        const_ready = sem("const_ready")
        v_ones_ready = sem("v_ones_ready")
        k_ones_ready = sem("k_ones_ready")
        th_ready = sem("th_ready")
        silu_ready = sem("silu_ready")
        modc_full = sem("modc_full")
        modc_ready = sem("modc_ready")
        gate_full = sem("gate_full")
        gate_step = sem("gate_step")
        gate_ready = sem("gate_ready")
        mod_stored = sem("mod_stored")
        x_loaded = sem("x_loaded")
        mpre_loaded = sem("mpre_loaded")
        stats1_step = sem("stats1_step")
        seeded1 = sem("seeded1")
        newton1_step = sem("newton1_step")
        rstd1_ready = sem("rstd1_ready")
        xn1_ready = sem("xn1_ready")
        xnT_full = sem("xnT_full")
        hT_done = sem("hT_done")
        q_full = sem("q_full")
        q_piece = sem("q_piece")
        k_full = sem("k_full")
        k_piece = sem("k_piece")
        v_full = sem("v_full")
        v_done = sem("v_done")
        q_stored = sem("q_stored")
        k_stored = sem("k_stored")
        stack_loaded = sem("stack_loaded")
        max_full = sem("max_full")
        max_read = sem("max_read")
        mT_full = sem("mT_full")
        m1_ready = sem("m1_ready")
        m2_ready = sem("m2_ready")
        m_stored = sem("m_stored")
        m_loaded = sem("m_loaded")
        sc_full = sem("sc_full")
        exp_done = sem("exp_done")
        masked = sem("masked")
        pv_full = sem("pv_full")
        oT_done = sem("oT_done")
        post_loaded = sem("post_loaded")
        gates_folded = sem("gates_folded")
        oTT_full = sem("oTT_full")
        rec_ready = sem("rec_ready")
        attn_done = sem("attn_done")
        aT_full = sem("aT_full")
        aT_done = sem("aT_done")
        o_full = sem("o_full")
        x1_done = sem("x1_done")
        stats2_step = sem("stats2_step")
        seeded2 = sem("seeded2")
        newton2_step = sem("newton2_step")
        rstd2_ready = sem("rstd2_ready")
        xn2_ready = sem("xn2_ready")
        xn2T_full = sem("xn2T_full")
        h2_done = sem("h2_done")
        diff_done = sem("diff_done")
        mixed = sem("mixed")
        kp_full = sem("kp_full")
        relu_done = sem("relu_done")
        act_done = sem("act_done")
        rp_full = sem("rp_full")
        tanh_done = sem("tanh_done")
        vp_full = sem("vp_full")
        y_done = sem("y_done")
        out_added = sem("out_added")
        out_stored = sem("out_stored")

        FREE = (PB, PA, MX[0], MX[1])

        block = ctx.enter_context(nc.Block())

        def later(count):
            return not isinstance(count, int) or count > 0

        def more(b):
            return not isinstance(b, int) or b + 2 < B

        def slots(e, prologue, half, epilogue):
            prologue()
            for i in range(SL):
                half(0, 0, i, True, False)
            with e.Fori(0, (B - 3) // 2) as pair:
                for k in range(2):
                    for i in range(SL):
                        half(2 * pair + 1 + k, (1 + k) % 2, i, False, False)
            for b in range(B - 3, B):
                for i in range(SL):
                    half(b, b % 2, i, False, b == B - 1)
            epilogue()

        def ring(par, i):
            return SL * par + i

        @block.sync
        def _(sp):
            sp.dma_start(cond_sb, cond.rearrange("(c p) b -> p c b", p=P)).then_inc(cond_loaded, 16)
            sp.dma_start(xin[:, :, :], x[0].rearrange("(t p) e -> p t e", p=P)).then_inc(x_loaded, 16)
            sp.dma_start(mod_sb, mod_w.rearrange("(c p) f -> p c f", p=P)).then_inc(modw_loaded, 16)
            for dst, src in ((qk_sb, qk_w), (v_sb, v_w), (o_sb, o_w), (r_sb, r_w), (k_sb, k_w), (c_sb, c_w)):
                sp.dma_start(dst[:, :, :], src.rearrange("(c p) f -> p c f", p=P)).then_inc(weights_loaded, 16)
            sp.dma_start(mu_sb[:, 0, :], mu_r).then_inc(weights_loaded, 16)
            sp.dma_start(mu_sb[:, 1, :], mu_k).then_inc(weights_loaded, 16)
            sp.wait_ge(modc_ready, 2)
            sp.dma_start(modc_dram.rearrange("b p k -> p b k"), modc).then_inc(mod_stored, 16)
            sp.wait_ge(mod_stored, 16)
            sp.dma_start(mpre[:, :], modc_dram[0]).then_inc(mpre_loaded, 16)
            sp.wait_ge(gate_ready, 1)
            sp.dma_start(gate_dram, gr[3]).then_inc(mod_stored, 16)

            def load_mpre(b):
                if later(EC * b):
                    sp.wait_ge(hT_done, EC * b)
                sp.dma_start(mpre[:, :], modc_dram[b]).then_inc(mpre_loaded, 16)

            def load_x(b):
                if later(EC * b):
                    sp.wait_ge(xnT_full, EC * b)
                sp.dma_start(xin[:, :, :], x[b].rearrange("(t p) e -> p t e", p=P)).then_inc(x_loaded, 16)
                load_mpre(b)

            def stack(n, r):
                sp.wait_ge(q_piece, NPC * (n + 1))
                sp.dma_start(q_dram[r].rearrange("a p q -> p a q"), qsp[:, :, :]).then_inc(q_stored, 16)
                sp.wait_ge(k_piece, NPC * (n + 1))
                sp.dma_start(k_dram[r].rearrange("a p q -> p a q"), ksp[:, :, :]).then_inc(k_stored, 16)
                sp.wait_ge(q_stored, 16 * (n + 1))
                for j, cnt, a in QR:
                    src = q_dram[r, a:a + cnt].rearrange("a (d h) q -> (a d) (h q)", h=HS)
                    sp.dma_start(Qs[r][D * j:D * (j + cnt), :, :].rearrange("p h q -> p (h q)"), src)\
                      .then_inc(stack_loaded, 16)
                sp.wait_ge(k_stored, 16 * (n + 1))
                for j, a in KR:
                    src = k_dram[r, a].rearrange("(d h) q -> d (h q)", h=HS)
                    sp.dma_start(Ks[r][D * j:D * (j + 1), :, :].rearrange("p h q -> p (h q)"), src)\
                      .then_inc(stack_loaded, 16)

            def max_rows(n, r):
                sp.wait_ge(m2_ready, n + 1)
                sp.dma_start(m_dram[r].rearrange("a h q -> h a q"), mT[:, :, :]).then_inc(m_stored, 16)
                sp.wait_ge(m_stored, 16 * (n + 1))
                sp.dma_start(Qs[r][KQ:KS, :, :].rearrange("p h q -> p (h q)"),
                             m_dram[r].rearrange("a h q -> a (h q)")).then_inc(m_loaded, 16)

            def post_loads(b):
                if later(b):
                    sp.wait_ge(out_added, b)
                sp.dma_start(gate_sb[:, :], bcast_rows(gate_dram, b, P)).then_inc(post_loaded, 16)
                sp.dma_start(mpost[:, :], modc_dram[b]).then_inc(post_loaded, 16)
                sp.dma_start(x1[:, :, :], x[b].rearrange("(t p) e -> p t e", p=P)).then_inc(post_loaded, 16)

            def prologue():
                load_x(1)
                stack(0, 0)
                sp.wait_ge(stack_loaded, 16 * (len(QR) + len(KR)))
                stack(1, 1)
                max_rows(0, 0)
                sp.wait_ge(mod_stored, 32)

            def half(b, par, i, first, last):
                n = SL * b + i
                if i == 0 and not first:
                    post_loads(b - 1)
                if not last:
                    stack(n + 2, ring(1 - par, i))
                if i == 0:
                    max_rows(n + 1, ring(par, 1))
                elif not last:
                    max_rows(n + 1, ring(1 - par, 0))
                if i == 0 and more(b):
                    load_x(b + 2)

            def epilogue():
                post_loads(B - 1)

            slots(sp, prologue, half, epilogue)
            sp.wait_ge(out_stored, 16 * B)

        @block.tensor
        def _(pe):
            mm = nc.tensor.matmul

            pe.wait_ge(modw_loaded, 16)
            pe.wait_ge(silu_ready, 1)
            for k, blk in enumerate((0, 1, 3, 4)):
                for co in range(EC):
                    for c in range(EC):
                        last = mm(PA[:, (EC * k + co) * B:(EC * k + co + 1) * B],
                                  mod_sb[:, c, blk * E + co * P:blk * E + (co + 1) * P], sT[:, c, :],
                                  start=(c == 0), stop=(c == EC - 1))
            last.then_inc(modc_full, 1)
            for k, blk in enumerate((2, 5)):
                for c in range(EC):
                    last = mm(PB[0:B, k * E:(k + 1) * E], sT[:, c, :], mod_sb[:, c, blk * E:(blk + 1) * E],
                              start=(c == 0), stop=(c == EC - 1))
            last.then_inc(gate_full, 1)
            pe.wait_ge(modc_ready, 2)
            pe.wait_ge(gate_step, 1)
            pe.wait_ge(const_ready, 1)

            def xn_transpose(b, c, bankt=PA):
                if c == 0:
                    pe.wait_ge(xn1_ready, b + 1)
                    if later(SL * b - 1):
                        pe.wait_ge(m2_ready, SL * b - 1)
                elif bankt is PA:
                    pe.wait_ge(hT_done, EC * b + c)
                for t in range(TT):
                    last = nc.tensor.transpose(bankt[:, t * P:(t + 1) * P], xin[:, t, c * P:(c + 1) * P], ident[:, :])
                last.then_inc(xnT_full, 1)

            def project(i, which, bankt, full):
                for c in range(EC):
                    last = mm(bankt[:, :], qk_sb[:, c, which * E + i * P:which * E + (i + 1) * P], hT[:, c, :],
                              start=(c == 0), stop=(c == EC - 1))
                last.then_inc(full, 1)

            def take_away(tile, j, bankt, full):
                mm(bankt[:, :], nidentb[:, :], tile[:, j, :], start=False, stop=True, skip_group_check=True)\
                    .then_inc(full, 1)

            def project_v(i, bankt):
                for t in range(TT):
                    for c in range(EC):
                        last = mm(bankt[:, t * P:(t + 1) * P], hT[:, c, t * P:(t + 1) * P],
                                  v_sb[:, c, i * P:(i + 1) * P], start=(c == 0), stop=(c == EC - 1))
                last.then_inc(v_full, 1)

            def q_step(b, i, j):
                n = SL * b + i
                if j > 0:
                    pe.wait_ge(q_piece, NPC * n + j)
                    take_away(qsp, j - 1, PA, q_full)
                else:
                    if i == 0:
                        pe.wait_ge(hT_done, EC * (b + 1))
                    else:
                        pe.wait_ge(v_done, n)
                        if later(n - 1):
                            pe.wait_ge(m2_ready, n - 1)
                    project(i, 0, PA, q_full)

            def k_step(n, i, j):
                if j > 0:
                    pe.wait_ge(k_piece, NPC * n + j)
                    take_away(ksp, j - 1, PA, k_full)
                else:
                    pe.wait_ge(q_piece, NPC * (n + 1))
                    project(i, 1, PA, k_full)

            def v_step(n, i):
                pe.wait_ge(k_piece, NPC * (n + 1))
                project_v(i, PA)

            def max_unit(n, r, u):
                if u == 0:
                    pe.wait_ge(stack_loaded, 16 * (len(QR) + len(KR)) * (n + 1))
                if later(GS * UM * n + u - 1):
                    pe.wait_ge(max_read, GS * UM * n + u - 1)
                bankt = MX[u % 2]
                h0, nh, qb = max_parts(u)
                w = (qb + 1) * P
                for k in range(nh):
                    mm(bankt[:, k * w:(k + 1) * w], Qs[r][0:KQ, h0 + k, qb * P:(qb + 1) * P],
                       Ks[r][0:KQ, h0 + k, 0:w], start=(k == 0), stop=False, skip_group_check=True)
                for k in range(nh):
                    last = mm(bankt[:, (k + 1) * w - P:(k + 1) * w], identb[:, :], maskb[:, :],
                              start=False, stop=(k == nh - 1), skip_group_check=True)
                last.then_inc(max_full, 1)

            def max_transpose(n):
                pe.wait_ge(max_read, GS * UM * (n + 1))
                pe.wait_ge(v_done, min(n + 2, SL * B) if isinstance(n, int) else n + 2)
                for qb in range(TT):
                    last = nc.tensor.transpose(PA[0:HS, qb * P:(qb + 1) * P], rmax[:, qb, :], ident[:, :])
                last.then_inc(mT_full, 1)

            def score_unit(n, r, u):
                if u == 0:
                    pe.wait_ge(m_loaded, 16 * (n + 1))
                if later(GS * UE * n + u - 1):
                    pe.wait_ge(exp_done, GS * UE * n + u - 1)
                at = 0
                for h, kb in score_parts(u):
                    w = T - kb * P
                    last = mm(ES[u % 2][:, at:at + w], Ks[r][:, h, kb * P:(kb + 1) * P], Qs[r][:, h, kb * P:T],
                              start=True, stop=True)
                    at += w
                last.then_inc(sc_full, 1)

            def pv(n, r, g):
                pe.wait_ge(v_done, n + 1)
                if later(GS * n + g - 1):
                    pe.wait_ge(oT_done, GS * n + g - 1)
                for kb in range(TT):
                    pe.wait_ge(masked, TT * (GS * n + g) + kb + 1)
                    w = T - kb * P
                    for h in range(HG):
                        last = mm(OT[g][CT * h:CT * (h + 1), kb * P:T], Va[r][:, kb, HG * g + h, :],
                                  PT[g][:, h, KBO[kb]:KBO[kb] + w], start=(kb == 0), stop=(kb == TT - 1))
                last.then_inc(pv_full, 1)

            def head_transpose(b, t, bankt=PB):
                if t == 0:
                    pe.wait_ge(oT_done, SL * GS * (b + 1))
                    if later(2 * b):
                        pe.wait_ge(y_done, 2 * b)
                elif bankt is PB:
                    pe.wait_ge(attn_done, TT * b + t)
                for g in range(SL * GS):
                    last = nc.tensor.transpose(bankt[:, g * P:(g + 1) * P], oT[:, g, t * P:(t + 1) * P], ident[:, :])
                last.then_inc(oTT_full, 1)

            def attn_transpose(b, c, bankt=PB):
                if c == 0:
                    pe.wait_ge(attn_done, TT * (b + 1))
                elif bankt is PB:
                    pe.wait_ge(aT_done, EC * b + c)
                for t in range(TT):
                    last = nc.tensor.transpose(bankt[:, t * P:(t + 1) * P], attn[:, t, c * P:(c + 1) * P], ident[:, :])
                last.then_inc(aT_full, 1)

            def token_product(actT, w, j, bankt):
                for t in (2 * j, 2 * j + 1):
                    for c in range(EC):
                        last = mm(bankt[:, (t % 2) * E:(t % 2 + 1) * E], actT[:, c, t * P:(t + 1) * P], w[:, c, :],
                                  start=(c == 0), stop=(c == EC - 1))
                return last

            def out_project(b, j, bankt=PB):
                if j == 0:
                    pe.wait_ge(aT_done, EC * (b + 1))
                    pe.wait_ge(gates_folded, 2 * b + 1)
                elif bankt is PB:
                    pe.wait_ge(x1_done, 2 * b + j)
                token_product(aT, og_sb, j, bankt).then_inc(o_full, 1)

            def xn2_transpose(b, c, bankt=PB):
                if c == 0:
                    pe.wait_ge(xn2_ready, b + 1)
                elif bankt is PB:
                    pe.wait_ge(h2_done, EC * b + c)
                for t in range(TT):
                    last = nc.tensor.transpose(bankt[:, t * P:(t + 1) * P], attn[:, t, c * P:(c + 1) * P], ident[:, :])
                last.then_inc(xn2T_full, 1)

            def key_project(b, co, bankt=PB):
                if co == 0:
                    pe.wait_ge(mixed, 2 * b + 1)
                elif bankt is PB:
                    pe.wait_ge(relu_done, EC * b + co)
                for c in range(EC):
                    last = mm(bankt[:, :], k_sb[:, c, co * P:(co + 1) * P], xk[:, c, :],
                              start=(c == 0), stop=(c == EC - 1))
                last.then_inc(kp_full, 1)

            def receptance_project(b, j, bankt=PB):
                if j == 0:
                    pe.wait_ge(mixed, 2 * b + 2)
                if bankt is PB and j == 0:
                    pe.wait_ge(relu_done, EC * (b + 1))
                elif bankt is PB:
                    pe.wait_ge(tanh_done, 2 * b + j)
                token_product(xr, r_sb, j, bankt).then_inc(rp_full, 1)

            def value_project(b, j, bankt=PB):
                if j == 0:
                    pe.wait_ge(tanh_done, 2 * (b + 1))
                    pe.wait_ge(act_done, EC * (b + 1))
                    pe.wait_ge(gates_folded, 2 * b + 2)
                elif bankt is PB:
                    pe.wait_ge(y_done, 2 * b + j)
                token_product(ka, cg_sb, j, bankt).then_inc(vp_full, 1)

            def pre_step(b, i, k):
                if i == 0 and k in XNT_AT:
                    xn_transpose(b, XNT_AT.index(k))
                elif k in Q_AT[i]:
                    q_step(b, i, Q_AT[i].index(k))
                elif k in K_AT[i]:
                    k_step(SL * b + i, i, K_AT[i].index(k))
                elif k == V_AT[i]:
                    v_step(SL * b + i, i)

            def post_step(b, p):
                if p in HEADT_AT:
                    head_transpose(b, HEADT_AT.index(p))
                elif p in ATTNT_AT:
                    attn_transpose(b, ATTNT_AT.index(p))
                elif p in OUT_AT:
                    out_project(b, OUT_AT.index(p))
                elif p in XN2T_AT:
                    xn2_transpose(b, XN2T_AT.index(p))
                elif p in KEY_AT:
                    key_project(b, KEY_AT.index(p))
                elif p in REC_AT:
                    receptance_project(b, REC_AT.index(p))
                elif p in VAL_AT:
                    value_project(b, VAL_AT.index(p))

            def prologue():
                for c in range(EC):
                    xn_transpose(0, c, (PA, PB)[c])
                pe.wait_ge(weights_loaded, 16 * 8)
                pe.wait_ge(hT_done, EC)
                project(0, 0, PA, q_full)
                project(0, 1, PB, k_full)
                for j in range(NPC - 1):
                    pe.wait_ge(q_piece, j + 1)
                    take_away(qsp, j, PA, q_full)
                    pe.wait_ge(k_piece, j + 1)
                    take_away(ksp, j, PB, k_full)
                pe.wait_ge(q_piece, NPC)
                project_v(0, PA)
                pe.wait_ge(k_piece, NPC)
                project(1, 0, PB, q_full)
                pe.wait_ge(v_done, 1)
                project(1, 1, PA, k_full)
                for j in range(NPC - 1):
                    pe.wait_ge(q_piece, NPC + j + 1)
                    take_away(qsp, j, PB, q_full)
                    pe.wait_ge(k_piece, NPC + j + 1)
                    take_away(ksp, j, PA, k_full)
                pe.wait_ge(q_piece, SL * NPC)
                project_v(1, PB)
                for u in range(GS * UM):
                    max_unit(0, 0, u)
                pe.wait_ge(k_piece, SL * NPC)
                max_transpose(0)
                pe.wait_ge(k_ones_ready, 1)
                pe.wait_ge(v_ones_ready, 1)

            def half(b, par, i, first, last):
                n = SL * b + i
                r, rn = ring(par, i), ring(par, 1) if i == 0 else ring(1 - par, 0)
                for k in range(NPOS):
                    g, u = divmod(k, UM)
                    if u < UE and SCORE_FIRST:
                        score_unit(n, r, UE * g + u)
                    if i == 0 or not last:
                        for m in max_units(k):
                            max_unit(n + 1, rn, m)
                    if u < UE and not SCORE_FIRST:
                        score_unit(n, r, UE * g + u)
                    if k == PV_BEFORE and not (first and i == 0):
                        pv(n - 1, (r - 1) % RING, 1)
                    if k == PV_THIS:
                        pv(n, r, 0)
                    if not last:
                        pre_step(b + 1, i, k)
                    if k == MAXT_AT[i] and (i == 0 or not last):
                        max_transpose(n + 1)
                    if not first:
                        post_step(b - 1, NPOS * i + k)

            def epilogue():
                pv(SL * B - 1, RING - 1, 1)
                for t in range(TT):
                    head_transpose(B - 1, t, FREE[t])
                for c in range(EC):
                    attn_transpose(B - 1, c, FREE[c])
                for j in range(2):
                    out_project(B - 1, j, FREE[j])
                for c in range(EC):
                    xn2_transpose(B - 1, c, FREE[c])
                for co in range(EC):
                    key_project(B - 1, co, FREE[co])
                for j in range(2):
                    receptance_project(B - 1, j, FREE[2 + j])
                for j in range(2):
                    value_project(B - 1, j, FREE[j])

            slots(pe, prologue, half, epilogue)

        @block.scalar
        def _(act):
            fn = nc.scalar.activation
            act.wait_ge(cond_loaded, 16)
            fn(th_sb, cond_sb, ACT.Tanh, scale=0.5).then_inc(th_ready, 1)

            def norm1(b):
                act.wait_ge(rstd1_ready, b + 1)
                for t in range(TT):
                    last = fn(xin[:, t, :], xin[:, t, :], ACT.Identity, bias=nm1[:, t:t + 1], scale=rs1[:, t:t + 1])
                last.then_inc(xn1_ready, 1)

            def modulate1(b, c, bankt=PA):
                act.wait_ge(xnT_full, EC * b + c + 1)
                act.wait_ge(mpre_loaded, 16 * (b + 1))
                if c == 0:
                    if later(SL * b):
                        act.wait_ge(v_full, SL * b)
                fn(hT[:, c, :], bankt[:, :], ACT.Identity, bias=mpre[:, c:c + 1], scale=mpre[:, EC + c:EC + c + 1])\
                    .then_inc(hT_done, 1)

            def piece(n, which, j, bankt=PA):
                full, done, tile, stored = ((q_full, q_piece, qsp, q_stored) if which == 0 else
                                            (k_full, k_piece, ksp, k_stored))
                act.wait_ge(full, NPC * n + j + 1)
                if j == 0:
                    if later(16 * n):
                        act.wait_ge(stored, 16 * n)
                fn(tile[:, j, :], bankt[:, :], ACT.Copy).then_inc(done, 1)

            def max_piece(n):
                act.wait_ge(mT_full, n + 1)
                if later(16 * n):
                    act.wait_ge(m_stored, 16 * n)
                fn(mT[:, 0, :], PA[0:HS, :], ACT.Copy, scale=-1.0).then_inc(m1_ready, 1)

            def exp_unit(n, u):
                g, v = divmod(u, UE)
                act.wait_ge(sc_full, GS * UE * n + u + 1)
                if v == 0:
                    if later(GS * n + g - 1):
                        act.wait_ge(pv_full, GS * n + g - 1)
                pair, w = divmod(v, 5)
                if w < 4:
                    h, part = 2 * pair + w // 2, w % 2
                    fn(PT[g][:, h, part * T:(part + 1) * T], ES[u % 2][:, :], ACT.Exp, scale=SCALE)\
                        .then_inc(exp_done, 1)
                else:
                    fn(PT[g][:, 2 * pair:2 * pair + 2, 2 * T:HT], ES[u % 2][:, :].rearrange("p (h q) -> p h q", h=2),
                       ACT.Exp, scale=SCALE).then_inc(exp_done, 1)

            def take_pv(n, b, i, g):
                act.wait_ge(pv_full, GS * n + g + 1)
                if later(TT * b):
                    act.wait_ge(oTT_full, TT * b)
                fn(oT[:, GS * i + g, :], OT[g][:, :], ACT.Copy).then_inc(oT_done, 1)

            def take_attn(b, c, bankt=PB):
                act.wait_ge(aT_full, EC * b + c + 1)
                fn(aT[:, c, :], bankt[:, :], ACT.Copy).then_inc(aT_done, 1)

            def norm2(b):
                act.wait_ge(rstd2_ready, b + 1)
                for t in range(TT):
                    last = fn(attn[:, t, :], x1[:, t, :], ACT.Identity, bias=nm2[:, t:t + 1], scale=rs2[:, t:t + 1])
                last.then_inc(xn2_ready, 1)

            def modulate2(b, c, bankt=PB):
                act.wait_ge(xn2T_full, EC * b + c + 1)
                if later(2 * b):
                    act.wait_ge(mixed, 2 * b)
                fn(h2[:, c, 1:T + 1], bankt[:, :], ACT.Identity, bias=mpost[:, 4 + c:5 + c],
                   scale=mpost[:, 6 + c:7 + c]).then_inc(h2_done, 1)

            def relu(b, c, bankt=PB):
                act.wait_ge(kp_full, EC * b + c + 1)
                if later(2 * b):
                    act.wait_ge(vp_full, 2 * b)
                fn(ka[:, c, :], bankt[:, :], ACT.Relu).then_inc(relu_done, 1)

            def receptance(b, j, bankt=PB):
                act.wait_ge(rp_full, 2 * b + j + 1)
                if later(16 * b):
                    act.wait_ge(out_stored, 16 * b)
                fn(y[:, 2 * j:2 * j + 2, :], bankt[:, :].rearrange("p (t e) -> p t e", t=2), ACT.Tanh, scale=0.5)\
                    .then_inc(tanh_done, 1)

            def pre_step(b, i, k):
                if i == 0 and k == NORM1_AT:
                    norm1(b)
                elif i == 0 and k in XNT_AT:
                    modulate1(b, XNT_AT.index(k))
                elif k in Q_AT[i] and k != Q_AT[i][1]:
                    piece(SL * b + i, 0, Q_AT[i].index(k))
                elif k in K_AT[i] and k != K_AT[i][1]:
                    piece(SL * b + i, 1, K_AT[i].index(k))

            def post_step(b, p):
                if p in ATTNT_AT:
                    take_attn(b, ATTNT_AT.index(p))
                elif p == NORM2_AT:
                    norm2(b)
                elif p in XN2T_AT:
                    modulate2(b, XN2T_AT.index(p))
                elif p in KEY_AT:
                    relu(b, KEY_AT.index(p))
                elif p in REC_AT:
                    receptance(b, REC_AT.index(p))

            def prologue():
                for c in range(EC):
                    if c == 0:
                        norm1(0)
                    modulate1(0, c, (PA, PB)[c])
                for i in range(SL):
                    for j in (0, 2):
                        piece(i, 0, j, (PA, PB)[i])
                        piece(i, 1, j, (PB, PA)[i])
                max_piece(0)

            def half(b, par, i, first, last):
                n = SL * b + i
                for k in range(NPOS):
                    g, u = divmod(k, UM)
                    if u < UE:
                        exp_unit(n, UE * g + u)
                    if k == PV_BEFORE and not (first and i == 0):
                        if i == 0:
                            take_pv(n - 1, b - 1, 1, 1)
                        else:
                            take_pv(n - 1, b, 0, 1)
                    if k == PV_THIS:
                        take_pv(n, b, i, 0)
                    if not last:
                        pre_step(b + 1, i, k)
                    if k == MAXT_AT[i] and (i == 0 or not last):
                        max_piece(n + 1)
                    if not first:
                        post_step(b - 1, NPOS * i + k)

            def epilogue():
                take_pv(SL * B - 1, B - 1, 1, 1)
                for c in range(EC):
                    take_attn(B - 1, c, FREE[c])
                norm2(B - 1)
                for c in range(EC):
                    modulate2(B - 1, c, FREE[c])
                for c in range(EC):
                    relu(B - 1, c, FREE[c])
                for j in range(2):
                    receptance(B - 1, j, FREE[2 + j])

            slots(act, prologue, half, epilogue)

        @block.vector
        def _(dve):
            v = nc.vector
            dve.wait_ge(th_ready, 1)
            v.scalar_tensor_tensor(out=sT, in0=th_sb, scalar=1.0, in1=cond_sb, op0=ALU.add, op1=ALU.mult)\
                .then_inc(silu_ready, 1)
            def stats(b, s, src, st, mv, nw, rs, step, seeded, used):
                if s == 0:
                    if later(b):
                        dve.wait_ge(used, b)
                    for t in range(TT):
                        last = v.bn_stats(st[:, t, :], src[:, t, :])
                    last.then_inc(step, 1)
                elif s == 1:
                    dve.wait_ge(step, 3 * b + 1)
                    v.memset(nw[:, 2, :], 0.0)
                    for t in range(TT):
                        last = v.bn_aggr(mv[:, t, :], st[:, t, :])
                    last.then_inc(step, 1)
                elif s == 2:
                    dve.wait_ge(step, 3 * b + 2)
                    v.tensor_scalar(nw[:, 0, :], mv[:, :, 1], EPS, None, ALU.add).then_inc(step, 1)
                else:
                    dve.wait_ge(step, 3 * b + 3)
                    v.tensor_scalar(nw[:, 1, :], nw[:, 0, :], -0.5, None, ALU.mult)
                    v.tensor_scalar(rs[:, :].bitcast(i32), nw[:, 0, :].bitcast(i32), -0.5, RSQRT_SEED, ALU.mult,
                                    ALU.add).then_inc(seeded, 1)

            def stats1(b, s):
                if s == 0:
                    dve.wait_ge(x_loaded, 16 * (b + 1))
                stats(b, s, xin, st1, mv1, nw1, rs1, stats1_step, seeded1, xn1_ready)

            def piece(n, which, j, bankt=PA):
                full, done, tile = (q_full, q_piece, qsp) if which == 0 else (k_full, k_piece, ksp)
                dve.wait_ge(full, NPC * n + j + 1)
                v.tensor_copy(tile[:, j, :], bankt[:, :]).then_inc(done, 1)

            def take_v(n, r, bankt=PA):
                dve.wait_ge(v_full, n + 1)
                if later(GS * (n - RING + 1)):
                    dve.wait_ge(pv_full, GS * (n - RING + 1))
                v.tensor_copy(Va[r][:, :, :, 0:D], bankt[:, :].rearrange("p (t h d) -> p t h d", t=TT, h=HS))\
                    .then_inc(v_done, 1)

            def max_unit(n, u):
                dve.wait_ge(max_full, GS * UM * n + u + 1)
                if u == 0:
                    if later(n):
                        dve.wait_ge(mT_full, n)
                h0, nh, qb = max_parts(u)
                w = (qb + 1) * P
                v.reduce_max(rmax[:, qb, h0:h0 + nh], MX[u % 2][:, 0:nh * w].rearrange("p (h k) -> p h k", h=nh),
                             axis=AX.X).then_inc(max_read, 1)

            def max_piece(n):
                dve.wait_ge(m1_ready, n + 1)
                dve.wait_ge(mT_full, n + 1)
                v.scalar_tensor_tensor(out=mT[:, 1, :], in0=PA[0:HS, :], scalar=-1.0, in1=mT[:, 0, :], op0=ALU.mult,
                                       op1=ALU.subtract).then_inc(m2_ready, 1)

            def normalise(b, t, bankt=PB):
                dve.wait_ge(oTT_full, TT * b + t + 1)
                heads = bankt[:, :].rearrange("p (h c) -> p h c", c=CT)
                v.reciprocal(rec[:, t, :], heads[:, :, D]).then_inc(rec_ready, 1)
                dve.wait_ge(rec_ready, TT * b + t + 1)
                if t == 0:
                    if later(EC * b):
                        dve.wait_ge(xn2T_full, EC * b)
                v.tensor_tensor(attn[:, t, :].rearrange("p (h d) -> p h d", d=D), heads[:, :, 0:D],
                                rec[:, t, :].unsqueeze(2).to_broadcast([P, H, D]), ALU.mult).then_inc(attn_done, 1)

            def add_attention(b, j, bankt=PB):
                dve.wait_ge(o_full, 2 * b + j + 1)
                dve.wait_ge(post_loaded, 48 * (b + 1))
                v.tensor_tensor(x1[:, 2 * j:2 * j + 2, :], bankt[:, :].rearrange("p (t e) -> p t e", t=2),
                                x1[:, 2 * j:2 * j + 2, :], ALU.add).then_inc(x1_done, 1)

            def stats2(b, s):
                if s == 0:
                    dve.wait_ge(x1_done, 2 * (b + 1))
                stats(b, s, x1, st2, mv2, nw2, rs2, stats2_step, seeded2, xn2_ready)

            def mix(b, which, dst):
                dve.wait_ge(diff_done, b + 1)
                dve.wait_ge(rp_full, 2 * b)
                for c in range(EC):
                    last = v.scalar_tensor_tensor(out=dst[:, c, :], in0=aT[:, c, :], scalar=mu_sb[:, which, c:c + 1],
                                                  in1=h2[:, c, 0:T], op0=ALU.mult, op1=ALU.add)
                last.then_inc(mixed, 1)

            def gate_value(b, j, bankt=PB):
                dve.wait_ge(vp_full, 2 * b + j + 1)
                dve.wait_ge(tanh_done, 2 * b + j + 1)
                yj = y[:, 2 * j:2 * j + 2, :]
                v.scalar_tensor_tensor(out=yj, in0=yj, scalar=1.0,
                                       in1=bankt[:, :].rearrange("p (t e) -> p t e", t=2), op0=ALU.add, op1=ALU.mult).then_inc(y_done, 1)

            def pre_step(b, i, k, r):
                n = SL * b + i
                if k == Q_AT[i][1]:
                    piece(n, 0, 1)
                elif k == K_AT[i][1]:
                    piece(n, 1, 1)
                elif k == V_AT[i]:
                    take_v(n, r)

            def post_step(b, p):
                if p in HEADT_AT:
                    normalise(b, HEADT_AT.index(p))
                elif p in OUT_AT:
                    add_attention(b, OUT_AT.index(p))
                elif p in STATS2_AT:
                    stats2(b, STATS2_AT.index(p))
                elif p == MIX_AT[0]:
                    mix(b, 1, xk)
                elif p == MIX_AT[1]:
                    mix(b, 0, xr)
                elif p in VAL_AT:
                    gate_value(b, VAL_AT.index(p))

            def prologue():
                for s in range(4):
                    stats1(0, s)
                dve.wait_ge(modc_full, 1)
                for k in range(4):
                    src = PA[:, EC * k * B:EC * (k + 1) * B].rearrange("p (c b) -> p b c", c=EC)
                    last = v.tensor_scalar(modc[:, :, EC * k:EC * (k + 1)], src, 0.5, float(k % 2), ALU.mult, ALU.add)
                    if k >= 2:
                        last.then_inc(modc_ready, 1)
                dve.wait_ge(gate_full, 1)
                v.tensor_scalar(gr[0], PB[0:B, :], 0.5, None, ALU.mult).then_inc(gate_step, 1)
                dve.wait_ge(gate_step, 1)
                v.tensor_scalar(gr[1], gr[0], -1.0, None, ALU.mult).then_inc(gate_step, 1)
                dve.wait_ge(gate_step, 2)
                v.scalar_tensor_tensor(out=gr[2], in0=gr[0], scalar=0.25, in1=gr[1], op0=ALU.max, op1=ALU.max)\
                    .then_inc(gate_step, 1)
                dve.wait_ge(gate_step, 3)
                v.tensor_scalar(gr[1], gr[0], 0.0, 2.0, ALU.is_ge, ALU.mult).then_inc(gate_step, 1)
                dve.wait_ge(gate_step, 4)
                v.scalar_tensor_tensor(out=gr[3], in0=gr[1], scalar=-1.0, in1=gr[2], op0=ALU.add, op1=ALU.mult)\
                    .then_inc(gate_step, 1)
                dve.wait_ge(gate_step, 5)
                v.tensor_scalar(gr[3][:, E:2 * E], gr[3][:, E:2 * E], 0.5, None, ALU.mult).then_inc(gate_ready, 1)
                v.memset(h2[:, :, 0:1], 0.0)
                for r in range(RING):
                    last = v.memset(Va[r][:, :, :, D:CT], 1.0)
                last.then_inc(v_ones_ready, 1)
                for i in range(SL):
                    piece(i, 0, 1, (PA, PB)[i])
                    piece(i, 1, 1, (PB, PA)[i])
                    take_v(i, i, (PA, PB)[i])
                dve.wait_ge(weights_loaded, 16 * 8)
                for s in range(4):
                    stats1(1, s)
                for u in range(GS * UM):
                    max_unit(0, u)
                max_piece(0)

            def half(b, par, i, first, last):
                n = SL * b + i
                for k in range(NPOS):
                    if i == 0 or not last:
                        for m in max_units(k):
                            max_unit(n + 1, m)
                    if not last:
                        pre_step(b + 1, i, k, ring(1 - par, i))
                    if i == 1 and k in STATS1_AT and more(b):
                        stats1(b + 2, STATS1_AT.index(k))
                    if k == MAXT_AT[i] and (i == 0 or not last):
                        max_piece(n + 1)
                    if not first:
                        post_step(b - 1, NPOS * i + k)

            def epilogue():
                for t in range(TT):
                    normalise(B - 1, t, FREE[t])
                for j in range(2):
                    add_attention(B - 1, j, FREE[j])
                for s in range(4):
                    stats2(B - 1, s)
                mix(B - 1, 1, xk)
                mix(B - 1, 0, xr)
                for j in range(2):
                    gate_value(B - 1, j, FREE[j])

            slots(dve, prologue, half, epilogue)

        @block.gpsimd
        def _(pool):
            g_ = nc.gpsimd
            g_.memset(ident[:, :], 0.0)
            g_.memset(pool_mark[:, :], 0.0)
            g_.memset(newton_c[:, 0, :], 1.5)
            g_.memset(newton_c[:, 1, :], -1.0)
            g_.memset(maskb[:, :], 0.0).then_inc(zeros_ready, 1)
            pool.wait_ge(zeros_ready, 1)
            g_.affine_select(out=ident[:, :], in_=ident[:, :], compare_op=ALU.not_equal, fill=1.0, base=0,
                             pattern=[[-1, P]], channel_multiplier=1).then_inc(ident_ready, 1)
            g_.affine_select(out=maskb[:, :], in_=maskb[:, :], compare_op=ALU.is_ge, fill=NEG, base=0,
                             pattern=[[-1, P]], channel_multiplier=1)
            pool.wait_ge(ident_ready, 1)
            g_.tensor_copy(identb[:, :], ident[:, :])
            g_.tensor_scalar(nidentb[:, :], ident[:, :], -1.0, None, ALU.mult).then_inc(const_ready, 1)

            def mask(n, g):
                pool.wait_ge(exp_done, UE * (GS * n + g + 1))
                g_.tensor_tensor(pool_mark[:, :], pool_mark[:, :], pool_mark[:, :], ALU.mult)
                for kb in range(TT):
                    blk = PT[g][:, :, KBO[kb]:KBO[kb] + P]
                    g_.affine_select(out=blk, in_=blk, compare_op=ALU.is_ge, fill=0.0, base=0,
                                     pattern=[[0, HG], [1, P]], channel_multiplier=-1).then_inc(masked, 1)

            def fold_gates(b):
                pool.wait_ge(post_loaded, 48 * (b + 1))
                if later(2 * b):
                    pool.wait_ge(o_full, 2 * b)
                ga = gate_sb[:, 0:E].unsqueeze(1).to_broadcast([P, EC, E])
                gb = gate_sb[:, E:2 * E].unsqueeze(1).to_broadcast([P, EC, E])
                g_.tensor_tensor(og_sb[:, :, :], o_sb[:, :, :], ga, ALU.mult).then_inc(gates_folded, 1)
                if later(2 * b):
                    pool.wait_ge(vp_full, 2 * b)
                g_.tensor_tensor(cg_sb[:, :, :], c_sb[:, :, :], gb, ALU.mult).then_inc(gates_folded, 1)

            def diff(b):
                pool.wait_ge(h2_done, EC * (b + 1))
                pool.wait_ge(o_full, 2 * (b + 1))
                g_.tensor_tensor(aT[:, :, :], h2[:, :, 1:T + 1], h2[:, :, 0:T], ALU.subtract)\
                    .then_inc(diff_done, 1)

            def square(b, c):
                pool.wait_ge(relu_done, EC * b + c + 1)
                g_.tensor_tensor(ka[:, c, :], ka[:, c, :], ka[:, c, :], ALU.mult).then_inc(act_done, 1)

            def finish(b):
                pool.wait_ge(y_done, 2 * (b + 1))
                g_.tensor_tensor(y[:, :, :], y[:, :, :], x1[:, :, :], ALU.add).then_inc(out_added, 1)
                pool.wait_ge(out_added, b + 1)
                pool.dma_start(out[b].rearrange("(t p) e -> p t e", p=P), y[:, :, :]).then_inc(out_stored, 16)

            def newton(b, mv, nw, rs, nm, seeded, step, ready):
                pool.wait_ge(seeded, b + 1)
                at = NEWTON_STEPS * b
                for _ in range(NEWTON):
                    g_.tensor_tensor(nw[:, 2, :], rs[:, :], rs[:, :], ALU.mult).then_inc(step, 1)
                    pool.wait_ge(step, at + 1)
                    g_.tensor_tensor(nw[:, 3, :], nw[:, 2, :], nw[:, 1, :], ALU.mult).then_inc(step, 1)
                    pool.wait_ge(step, at + 2)
                    g_.tensor_tensor(nw[:, 2, :], nw[:, 3, :], newton_c[:, 0, :], ALU.add).then_inc(step, 1)
                    pool.wait_ge(step, at + 3)
                    g_.tensor_tensor(rs[:, :], rs[:, :], nw[:, 2, :], ALU.mult).then_inc(step, 1)
                    pool.wait_ge(step, at + 4)
                    at = at + 4
                g_.tensor_tensor(nw[:, 3, :], mv[:, :, 0], rs[:, :], ALU.mult).then_inc(step, 1)
                pool.wait_ge(step, at + 1)
                g_.tensor_tensor(nm[:, :], nw[:, 3, :], newton_c[:, 1, :], ALU.mult).then_inc(ready, 1)

            def newton1(b):
                newton(b, mv1, nw1, rs1, nm1, seeded1, newton1_step, rstd1_ready)

            def post_step(b, p):
                if p == STATS2_AT[-1]:
                    newton(b, mv2, nw2, rs2, nm2, seeded2, newton2_step, rstd2_ready)
                if p == FOLD_AT:
                    fold_gates(b)
                if p == DIFF_AT:
                    diff(b)
                if p in KEY_AT:
                    square(b, KEY_AT.index(p))
                if p == VAL_AT[-1]:
                    finish(b)

            def prologue():
                newton1(0)
                pool.wait_ge(rstd1_ready, 1)
                for r in range(RING):
                    last = g_.memset(Ks[r][KQ:KS, :, :], 1.0)
                last.then_inc(k_ones_ready, 1)
                pool.wait_ge(k_ones_ready, 1)
                pool.wait_ge(weights_loaded, 16 * 8)
                newton1(1)

            def half(b, par, i, first, last):
                n = SL * b + i
                for k in range(NPOS):
                    if k == MASK_AT[0]:
                        mask(n, 0)
                    if k == MASK_AT[1]:
                        mask(n, 1)
                    if i == 1 and k == STATS1_AT[-1] and more(b):
                        newton1(b + 2)
                    if not first:
                        post_step(b - 1, NPOS * i + k)

            def epilogue():
                for p in range(SL * NPOS):
                    post_step(B - 1, p)

            slots(pool, prologue, half, epilogue)


def sb_view(tile, P, a, n):
    flat = tile[:, :, :].rearrange("p a b -> p (a b)")
    return flat[:, 0:a * n].rearrange("p (a n) -> p a n", a=a)


def bcast_rows(dram, b, P):
    return dram[b].unsqueeze(0).to_broadcast([P, dram.shape[1]])


def max_parts(u):
    g, v = divmod(u, 11)
    if v < 8:
        return 4 * g + v // 2, 1, 3 - v % 2
    if v < 10:
        return 4 * g + 2 * (v - 8), 2, 1
    return 4 * g, 4, 0


def score_parts(u):
    pair, w = divmod(u, 5)
    if w < 4:
        h = 2 * pair + w // 2
        return [(h, 0)] if w % 2 == 0 else [(h, 1), (h, 3)]
    return [(2 * pair, 2), (2 * pair + 1, 2)]


def kernel(**inputs):
    import numpy as _np
    import concourse.bacc as _bacc
    from concourse import mybir as _mybir
    from concourse.bass_utils import run_bass_kernel_spmd as _run

    a = {k: _np.asarray(v) for k, v in inputs.items()}
    E, D, H = 256, 16, 16
    in_w = a["L0_attn_in_proj_weight"].T
    qk = in_w[:, 0:2 * E].reshape(E, 2, 2, H // 2, D).transpose(0, 1, 2, 4, 3).reshape(E, 2 * E)
    arrays = {
        "x": a["L0_attn_query"], "qk_w": qk, "v_w": in_w[:, 2 * E:3 * E], "o_w": a["L0_attn_out_proj_weight"].T,
        "r_w": a["L0_ffn_W_r"].T, "k_w": a["L0_ffn_W_k"].T, "c_w": a["L0_ffn_W_v"].T,
        "mu_r": a["L0_ffn_mu_r"].reshape(2, 128).T, "mu_k": a["L0_ffn_mu_k"].reshape(2, 128).T,
        "cond": a["L0_c"].T, "mod_w": a["L0_wmod"],
    }
    arrays = {k: _np.ascontiguousarray(v) for k, v in arrays.items()}
    nc = _bacc.Bacc("TRN2", target_bir_lowering=False, num_devices=1)
    args = [nc.dram_tensor(k, v.shape, _mybir.dt.from_np(v.dtype), kind="ExternalInput").ap()
            for k, v in arrays.items()]
    out = nc.dram_tensor("out", a["L0_attn_query"].shape, _mybir.dt.float32, kind="ExternalOutput").ap()
    adaln_attention_channel_mix_kernel(nc, *args, out)
    r = _run(nc, [arrays], core_ids=[0])
    return r.results[0]["out"]
```

```python
import concourse.bass as bass
from concourse import mybir
from contextlib import ExitStack


def adaln_attention_channel_mix_kernel(nc, x, qk_w, v_w, o_w, r_w, k_w, c_w, mu_r, mu_k, cond, mod_w, out):
    f32, bf16, i32 = mybir.dt.float32, mybir.dt.bfloat16, mybir.dt.int32
    ALU, ACT, AX = mybir.AluOpType, mybir.ActivationFunctionType, mybir.AxisListType

    B, T, E = x.shape
    P = 128
    TT = T // P
    EC = E // P
    H, D = 16, 16
    HS = P // D
    SL = H // HS
    HG = 4
    GS = HS // HG
    CT = 32
    NPC = 3
    KQ = 6 * D
    KS = KQ + 2
    RING = 4
    HT = sum(T - kb * P for kb in range(TT))
    SCALE = 1.0 / D ** 0.5
    EPS = 1e-5
    RSQRT_SEED = float(0x5f3759df)
    NEWTON = 3
    NEWTON_STEPS = 4 * NEWTON + 1
    NEG = -1e30
    MXN = 3
    UM = 11
    UE = 10
    KBO = [0, T, 2 * T, T + 384]
    QR, KR = [(0, 3, 0), (3, 2, 0), (5, 1, 0)], [(0, 0), (1, 0), (2, 0), (3, 1), (4, 1), (5, 2)]

    NPOS = GS * UM
    MAX_COUNTS = ((1, 1, 2, 2, 1, 1, 1, 2, 1, 1, 2, 1, 1, 3, 1, 1, 0, 0, 0, 0, 0, 0),
                  (2, 0, 2, 0, 3, 1, 1, 2, 1, 2, 1, 1, 1, 2, 1, 2, 0, 0, 0, 0, 0, 0))
    EXP_COUNTS = ((1, 1, 1, 0, 1, 1, 1, 1, 1, 1, 1, 1, 1, 1, 0, 1, 1, 1, 1, 1, 1, 1),
                  (1, 1, 1, 0, 1, 1, 1, 1, 1, 1, 0, 2, 1, 1, 0, 1, 1, 2, 0, 2, 0, 1))
    MAXT_AT, EXP_TAIL = (17, 19), 2
    PV_BEFORE, PV_THIS, MASK_BEFORE, MASK_THIS = (6, 6), (21, 21), (3, 2), (14, 14)
    STATS1_AT, NORM1_AT, XNT_AT = (13, 15, 17, 19), 20, (2, 4)
    Q_AT, K_AT, V_AT = ((5, 6, 7), (3, 5, 7)), ((11, 12, 13), (9, 12, 15)), (16, 16)
    FOLD_AT, HEADT_AT, ATTNT_AT, OUT_AT = 6, (8, 10, 11, 12), (13, 15), (16, 19)
    STATS2_AT, NORM2_AT, XN2T_AT, DIFF_AT = (20, 21, 22, 23), 26, (28, 30), 31
    MIX_AT, KEY_AT, REC_AT, VAL_AT = (32, 33), (34, 36), (37, 40), (41, 43)
    POST_TAIL = max(0, VAL_AT[-1] + 1 - SL * NPOS)

    def max_units(i, k):
        at = sum(MAX_COUNTS[i][:k])
        return range(at, at + MAX_COUNTS[i][k])

    def exp_units(i, k):
        at = sum(EXP_COUNTS[i][:k])
        return [(1, c + GS * UE - EXP_TAIL) if c < EXP_TAIL else (0, c - EXP_TAIL)
                for c in range(at, at + EXP_COUNTS[i][k])]

    gate_dram = nc.dram_tensor("gate_rows", [B, 2 * E], f32, kind="Internal").ap()
    modc_dram = nc.dram_tensor("mod_columns", [B, P, 8], f32, kind="Internal").ap()
    q_dram = nc.dram_tensor("q_pieces", [RING, NPC, P, T], bf16, kind="Internal").ap()
    k_dram = nc.dram_tensor("k_pieces", [RING, NPC, P, T], bf16, kind="Internal").ap()
    m_dram = nc.dram_tensor("max_pieces", [RING, 2, HS, T], bf16, kind="Internal").ap()

    ctx = ExitStack()
    with ctx:
        def sb(name, shape, dt=f32):
            return ctx.enter_context(nc.sbuf_tensor(name, shape, dt))

        def sem(name):
            return ctx.enter_context(nc.semaphore(name))

        qk_sb = sb("qk_sb", [P, EC, 2 * E])
        v_sb = sb("v_sb", [P, EC, E])
        o_sb = sb("o_sb", [P, EC, E])
        r_sb = sb("r_sb", [P, EC, E])
        k_sb = sb("k_sb", [P, EC, E])
        c_sb = sb("c_sb", [P, EC, E])
        og_sb = sb("og_sb", [P, EC, E])
        cg_sb = sb("cg_sb", [P, EC, E])
        mu_sb = sb("mu_sb", [P, 2, EC])
        gate_sb = sb("gate_sb", [P, 2 * E])
        mpre = sb("mpre", [P, 8])
        mpost = sb("mpost", [P, 8])
        ident = sb("ident", [P, P])
        identb = sb("identb", [P, P], bf16)
        nidentb = sb("nidentb", [P, P], bf16)
        maskb = sb("maskb", [P, P], bf16)
        xin = sb("xin", [P, TT, E])
        st1 = sb("st1", [P, TT, 6])
        mv1 = sb("mv1", [P, TT, 2])
        nw1 = sb("nw1", [P, 4, TT])
        rs1 = sb("rs1", [P, TT])
        nm1 = sb("nm1", [P, TT])
        hT = sb("hT", [P, EC, T])
        qsp = sb("qsp", [P, NPC, T], bf16)
        ksp = sb("ksp", [P, NPC, T], bf16)
        Qs = [sb(f"Qs{r}", [KS, HS, T], bf16) for r in range(RING)]
        Ks = [sb(f"Ks{r}", [KS, HS, T], bf16) for r in range(RING)]
        Va = [sb(f"Va{r}", [P, TT, HS, CT]) for r in range(RING)]
        rmax = sb("rmax", [P, TT, HS])
        mT = sb("mT", [HS, 2, T], bf16)
        PT = [sb(f"PT{g}", [P, HG, HT]) for g in range(GS)]
        oT = sb("oT", [P, SL * GS, T])
        pool_mark = sb("pool_mark", [P, 1])
        newton_c = sb("newton_c", [P, 2, TT])
        rec = sb("rec", [P, TT, H])
        attn = sb("attn", [P, TT, E])
        aT = sb("aT", [P, EC, T])
        x1 = sb("x1", [P, TT, E])
        st2 = sb("st2", [P, TT, 6])
        mv2 = sb("mv2", [P, TT, 2])
        nw2 = sb("nw2", [P, 4, TT])
        rs2 = sb("rs2", [P, TT])
        nm2 = sb("nm2", [P, TT])
        h2 = sb("h2", [P, EC, T + 1])
        xr = sb("xr", [P, EC, T])
        xk = sb("xk", [P, EC, T])
        ka = sb("ka", [P, EC, T])
        y = sb("y", [P, TT, E])
        mod_sb = sb_view(PT[0], P, EC, 6 * E)
        cond_sb = y[:, 0, 0:EC * B].rearrange("p (c b) -> p c b", c=EC)
        th_sb = y[:, 1, 0:EC * B].rearrange("p (c b) -> p c b", c=EC)
        sT = y[:, 2, 0:EC * B].rearrange("p (c b) -> p c b", c=EC)
        gr = [xr[0:B, 0, :], xr[0:B, 1, :], xk[0:B, 0, :], xk[0:B, 1, :]]
        modc = ka[:, 0, 0:B * 8].rearrange("p (b k) -> p b k", k=8)

        def bank(name):
            return ctx.enter_context(nc.psum_tensor(name, [P, 512], f32))

        ES = [bank(f"scores{i}") for i in range(2)]
        MX = [bank(f"maxed{i}") for i in range(MXN)]
        MT = MX[GS * UM % MXN]
        OT = bank("pv_bank")
        PA = bank("pre_bank")
        PB = bank("post_bank")

        weights_loaded = sem("weights_loaded")
        cond_loaded = sem("cond_loaded")
        modw1_loaded = sem("modw1_loaded")
        modw2_loaded = sem("modw2_loaded")
        zeros_ready = sem("zeros_ready")
        ident_ready = sem("ident_ready")
        const_ready = sem("const_ready")
        v_ones_ready = sem("v_ones_ready")
        k_ones_ready = sem("k_ones_ready")
        th_ready = sem("th_ready")
        silu_ready = sem("silu_ready")
        modc_full = sem("modc_full")
        modc_ready = sem("modc_ready")
        gate_full = sem("gate_full")
        gate_step = sem("gate_step")
        gate_ready = sem("gate_ready")
        mod_stored = sem("mod_stored")
        x_loaded = sem("x_loaded")
        mpre_loaded = sem("mpre_loaded")
        stats1_step = sem("stats1_step")
        seeded1 = sem("seeded1")
        newton1_step = sem("newton1_step")
        rstd1_ready = sem("rstd1_ready")
        xn1_ready = sem("xn1_ready")
        xnT_full = sem("xnT_full")
        hT_done = sem("hT_done")
        q_full = sem("q_full")
        q_piece = sem("q_piece")
        k_full = sem("k_full")
        k_piece = sem("k_piece")
        v_full = sem("v_full")
        v_done = sem("v_done")
        q_stored = sem("q_stored")
        k_stored = sem("k_stored")
        stack_loaded = sem("stack_loaded")
        max_full = sem("max_full")
        max_read = sem("max_read")
        mT_full = sem("mT_full")
        m1_ready = sem("m1_ready")
        m2_ready = sem("m2_ready")
        m_stored = sem("m_stored")
        m_loaded = sem("m_loaded")
        sc_full = sem("sc_full")
        exp_done = sem("exp_done")
        masked = sem("masked")
        pv_full = sem("pv_full")
        oT_done = sem("oT_done")
        post_loaded = sem("post_loaded")
        gates_folded = sem("gates_folded")
        oTT_full = sem("oTT_full")
        rec_ready = sem("rec_ready")
        attn_done = sem("attn_done")
        aT_full = sem("aT_full")
        aT_done = sem("aT_done")
        o_full = sem("o_full")
        x1_done = sem("x1_done")
        stats2_step = sem("stats2_step")
        seeded2 = sem("seeded2")
        newton2_step = sem("newton2_step")
        rstd2_ready = sem("rstd2_ready")
        xn2_ready = sem("xn2_ready")
        xn2T_full = sem("xn2T_full")
        h2_done = sem("h2_done")
        diff_done = sem("diff_done")
        mixed = sem("mixed")
        kp_full = sem("kp_full")
        relu_done = sem("relu_done")
        act_done = sem("act_done")
        rp_full = sem("rp_full")
        tanh_done = sem("tanh_done")
        vp_full = sem("vp_full")
        y_done = sem("y_done")
        out_added = sem("out_added")
        out_stored = sem("out_stored")

        FREE = (PB, PA, MX[0], MX[1])

        block = ctx.enter_context(nc.Block())

        def later(count):
            return not isinstance(count, int) or count > 0

        def more(b):
            return not isinstance(b, int) or b + 2 < B

        def from_batch(b, m):
            return not isinstance(b, int) or b >= m

        def slots(e, prologue, half, epilogue):
            prologue()
            for b in range(2):
                for i in range(SL):
                    half(b, b, i, b == 0, False)
            with e.Fori(0, (B - 4) // 2) as pair:
                for k in range(2):
                    for i in range(SL):
                        half(2 * pair + 2 + k, k, i, False, False)
            for b in range(B - 2, B):
                for i in range(SL):
                    half(b, b % 2, i, False, b == B - 1)
            epilogue()

        def ring(par, i):
            return SL * par + i

        @block.sync
        def _(sp):
            sp.dma_start(cond_sb, cond.rearrange("(c p) b -> p c b", p=P)).then_inc(cond_loaded, 16)
            sp.dma_start(xin[:, :, :], x[0].rearrange("(t p) e -> p t e", p=P)).then_inc(x_loaded, 16)
            for cols, loaded in ((slice(0, 2 * E), modw1_loaded), (slice(2 * E, 6 * E), modw2_loaded)):
                sp.dma_start(mod_sb[:, :, cols], mod_w[:, cols].rearrange("(c p) f -> p c f", p=P)).then_inc(loaded, 16)
            for dst, src in ((qk_sb, qk_w), (v_sb, v_w), (o_sb, o_w), (r_sb, r_w), (k_sb, k_w), (c_sb, c_w)):
                sp.dma_start(dst[:, :, :], src.rearrange("(c p) f -> p c f", p=P)).then_inc(weights_loaded, 16)
            sp.dma_start(mu_sb[:, 0, :], mu_r).then_inc(weights_loaded, 16)
            sp.dma_start(mu_sb[:, 1, :], mu_k).then_inc(weights_loaded, 16)

            def load_mpre(b):
                if later(EC * b):
                    sp.wait_ge(hT_done, EC * b)
                sp.dma_start(mpre[:, :], modc_dram[b]).then_inc(mpre_loaded, 16)

            def load_x(b):
                if later(EC * b):
                    sp.wait_ge(xnT_full, EC * b)
                sp.dma_start(xin[:, :, :], x[b].rearrange("(t p) e -> p t e", p=P)).then_inc(x_loaded, 16)

            def stack(n, r):
                sp.wait_ge(q_piece, NPC * (n + 1))
                sp.dma_start(q_dram[r].rearrange("a p q -> p a q"), qsp[:, :, :]).then_inc(q_stored, 16)
                sp.wait_ge(k_piece, NPC * (n + 1))
                sp.dma_start(k_dram[r].rearrange("a p q -> p a q"), ksp[:, :, :]).then_inc(k_stored, 16)
                sp.wait_ge(q_stored, 16 * (n + 1))
                for j, cnt, a in QR:
                    src = q_dram[r, a:a + cnt].rearrange("a (d h) q -> (a d) (h q)", h=HS)
                    sp.dma_start(Qs[r][D * j:D * (j + cnt), :, :].rearrange("p h q -> p (h q)"), src)\
                      .then_inc(stack_loaded, 16)
                sp.wait_ge(k_stored, 16 * (n + 1))
                for j, a in KR:
                    src = k_dram[r, a].rearrange("(d h) q -> d (h q)", h=HS)
                    sp.dma_start(Ks[r][D * j:D * (j + 1), :, :].rearrange("p h q -> p (h q)"), src)\
                      .then_inc(stack_loaded, 16)

            def max_rows(n, r):
                sp.wait_ge(m2_ready, n + 1)
                sp.dma_start(m_dram[r].rearrange("a h q -> h a q"), mT[:, :, :]).then_inc(m_stored, 16)
                sp.wait_ge(m_stored, 16 * (n + 1))
                sp.dma_start(Qs[r][KQ:KS, :, :].rearrange("p h q -> p (h q)"),
                             m_dram[r].rearrange("a h q -> a (h q)")).then_inc(m_loaded, 16)

            def post_loads(b):
                if later(b):
                    sp.wait_ge(out_added, b)
                sp.dma_start(gate_sb[:, :], bcast_rows(gate_dram, b, P)).then_inc(post_loaded, 16)
                sp.dma_start(mpost[:, :], modc_dram[b]).then_inc(post_loaded, 16)
                sp.dma_start(x1[:, :, :], x[b].rearrange("(t p) e -> p t e", p=P)).then_inc(post_loaded, 16)

            def prologue():
                load_x(1)
                stack(0, 0)
                sp.wait_ge(stack_loaded, 16 * (len(QR) + len(KR)))
                stack(1, 1)
                max_rows(0, 0)
                sp.wait_ge(modc_ready, 4)
                sp.dma_start(modc_dram.rearrange("b p k -> p b k"), modc).then_inc(mod_stored, 16)
                sp.wait_ge(mod_stored, 16)
                load_mpre(1)
                sp.wait_ge(gate_ready, 1)
                sp.dma_start(gate_dram, gr[3]).then_inc(mod_stored, 16)
                sp.wait_ge(mod_stored, 32)

            def half(b, par, i, first, last):
                n = SL * b + i
                if i == 0 and not first:
                    post_loads(b - 1)
                if not last:
                    stack(n + 2, ring(1 - par, i))
                if i == 0:
                    max_rows(n + 1, ring(par, 1))
                elif not last:
                    max_rows(n + 1, ring(1 - par, 0))
                if i == 0 and more(b):
                    load_x(b + 2)
                    load_mpre(b + 2)

            def epilogue():
                post_loads(B - 1)

            slots(sp, prologue, half, epilogue)
            sp.wait_ge(out_stored, 16 * B)

        @block.tensor
        def _(pe):
            mm = nc.tensor.matmul

            def mod_columns(part, bankt):
                pe.wait_ge((modw1_loaded, modw2_loaded)[part], 16)
                for k in range(2):
                    for co in range(EC):
                        for c in range(EC):
                            at = (3 * part + k) * E + co * P
                            last = mm(bankt[:, (EC * k + co) * B:(EC * k + co + 1) * B], mod_sb[:, c, at:at + P],
                                      sT[:, c, :], start=(c == 0), stop=(c == EC - 1))
                last.then_inc(modc_full, 1)

            pe.wait_ge(silu_ready, 1)
            mod_columns(0, PA)
            pe.wait_ge(modc_ready, 2)
            pe.wait_ge(const_ready, 1)

            def xn_transpose(b, c, bankt=PA):
                if c == 0:
                    pe.wait_ge(xn1_ready, b + 1)
                    if later(SL * b):
                        pe.wait_ge(v_done, SL * b)
                elif bankt is PA:
                    pe.wait_ge(hT_done, EC * b + c)
                for t in range(TT):
                    last = nc.tensor.transpose(bankt[:, t * P:(t + 1) * P], xin[:, t, c * P:(c + 1) * P], ident[:, :])
                last.then_inc(xnT_full, 1)

            def project(i, which, bankt, full):
                for c in range(EC):
                    last = mm(bankt[:, :], qk_sb[:, c, which * E + i * P:which * E + (i + 1) * P], hT[:, c, :],
                              start=(c == 0), stop=(c == EC - 1))
                last.then_inc(full, 1)

            def take_away(tile, j, bankt, full):
                mm(bankt[:, :], nidentb[:, :], tile[:, j, :], start=False, stop=True, skip_group_check=True)\
                    .then_inc(full, 1)

            def project_v(i, bankt):
                for t in range(TT):
                    for c in range(EC):
                        last = mm(bankt[:, t * P:(t + 1) * P], hT[:, c, t * P:(t + 1) * P],
                                  v_sb[:, c, i * P:(i + 1) * P], start=(c == 0), stop=(c == EC - 1))
                last.then_inc(v_full, 1)

            def q_step(b, i, j):
                n = SL * b + i
                if j > 0:
                    pe.wait_ge(q_piece, NPC * n + j)
                    take_away(qsp, j - 1, PA, q_full)
                else:
                    if i == 0:
                        pe.wait_ge(hT_done, EC * (b + 1))
                    else:
                        pe.wait_ge(v_done, n)
                    project(i, 0, PA, q_full)

            def k_step(n, i, j):
                if j > 0:
                    pe.wait_ge(k_piece, NPC * n + j)
                    take_away(ksp, j - 1, PA, k_full)
                else:
                    pe.wait_ge(q_piece, NPC * (n + 1))
                    project(i, 1, PA, k_full)

            def v_step(n, i):
                pe.wait_ge(k_piece, NPC * (n + 1))
                project_v(i, PA)

            def max_unit(n, r, u):
                if u == 0:
                    pe.wait_ge(stack_loaded, 16 * (len(QR) + len(KR)) * (n + 1))
                if MX[u % MXN] is MT and u < MXN and later(n):
                    pe.wait_ge(m2_ready, n)
                if later(GS * UM * n + max(u - MXN + 1, 0)):
                    pe.wait_ge(max_read, GS * UM * n + max(u - MXN + 1, 0))
                bankt = MX[u % MXN]
                h0, nh, qb = max_parts(u)
                w = (qb + 1) * P
                for k in range(nh):
                    mm(bankt[:, k * w:(k + 1) * w], Qs[r][0:KQ, h0 + k, qb * P:(qb + 1) * P],
                       Ks[r][0:KQ, h0 + k, 0:w], start=(k == 0), stop=False, skip_group_check=True)
                for k in range(nh):
                    last = mm(bankt[:, (k + 1) * w - P:(k + 1) * w], identb[:, :], maskb[:, :],
                              start=False, stop=(k == nh - 1), skip_group_check=True)
                last.then_inc(max_full, 1)

            def max_transpose(n):
                pe.wait_ge(max_read, GS * UM * (n + 1))
                for qb in range(TT):
                    last = nc.tensor.transpose(MT[0:HS, qb * P:(qb + 1) * P], rmax[:, qb, :], ident[:, :])
                last.then_inc(mT_full, 1)

            def score_unit(n, r, u):
                if u == 0:
                    pe.wait_ge(m_loaded, 16 * (n + 1))
                if later(GS * UE * n + u - 1):
                    pe.wait_ge(exp_done, GS * UE * n + u - 1)
                at = 0
                for h, kb in score_parts(u):
                    w = T - kb * P
                    last = mm(ES[u % 2][:, at:at + w], Ks[r][:, h, kb * P:(kb + 1) * P], Qs[r][:, h, kb * P:T],
                              start=True, stop=True)
                    at += w
                last.then_inc(sc_full, 1)

            def pv(n, r, g):
                pe.wait_ge(v_done, n + 1)
                if later(GS * n + g):
                    pe.wait_ge(oT_done, GS * n + g)
                for kb in range(TT):
                    pe.wait_ge(masked, TT * (GS * n + g) + kb + 1)
                    w = T - kb * P
                    for h in range(HG):
                        last = mm(OT[CT * h:CT * (h + 1), kb * P:T], Va[r][:, kb, HG * g + h, :],
                                  PT[g][:, h, KBO[kb]:KBO[kb] + w], start=(kb == 0), stop=(kb == TT - 1))
                last.then_inc(pv_full, 1)

            def head_transpose(b, t, bankt=PB):
                if t == 0:
                    pe.wait_ge(oT_done, SL * GS * (b + 1))
                    if later(2 * b):
                        pe.wait_ge(y_done, 2 * b)
                elif bankt is PB:
                    pe.wait_ge(attn_done, TT * b + t)
                for g in range(SL * GS):
                    last = nc.tensor.transpose(bankt[:, g * P:(g + 1) * P], oT[:, g, t * P:(t + 1) * P], ident[:, :])
                last.then_inc(oTT_full, 1)

            def attn_transpose(b, c, bankt=PB):
                if c == 0:
                    pe.wait_ge(attn_done, TT * (b + 1))
                elif bankt is PB:
                    pe.wait_ge(aT_done, EC * b + c)
                for t in range(TT):
                    last = nc.tensor.transpose(bankt[:, t * P:(t + 1) * P], attn[:, t, c * P:(c + 1) * P], ident[:, :])
                last.then_inc(aT_full, 1)

            def token_product(actT, w, j, bankt):
                for t in (2 * j, 2 * j + 1):
                    for c in range(EC):
                        last = mm(bankt[:, (t % 2) * E:(t % 2 + 1) * E], actT[:, c, t * P:(t + 1) * P], w[:, c, :],
                                  start=(c == 0), stop=(c == EC - 1))
                return last

            def out_project(b, j, bankt=PB):
                if j == 0:
                    pe.wait_ge(aT_done, EC * (b + 1))
                    pe.wait_ge(gates_folded, 2 * b + 1)
                elif bankt is PB:
                    pe.wait_ge(x1_done, 2 * b + j)
                token_product(aT, og_sb, j, bankt).then_inc(o_full, 1)

            def xn2_transpose(b, c, bankt=PB):
                if c == 0:
                    pe.wait_ge(xn2_ready, b + 1)
                elif bankt is PB:
                    pe.wait_ge(h2_done, EC * b + c)
                for t in range(TT):
                    last = nc.tensor.transpose(bankt[:, t * P:(t + 1) * P], attn[:, t, c * P:(c + 1) * P], ident[:, :])
                last.then_inc(xn2T_full, 1)

            def key_project(b, co, bankt=PB):
                if co == 0:
                    pe.wait_ge(mixed, 2 * b + 1)
                elif bankt is PB:
                    pe.wait_ge(relu_done, EC * b + co)
                for c in range(EC):
                    last = mm(bankt[:, :], k_sb[:, c, co * P:(co + 1) * P], xk[:, c, :],
                              start=(c == 0), stop=(c == EC - 1))
                last.then_inc(kp_full, 1)

            def receptance_project(b, j, bankt=PB):
                if j == 0:
                    pe.wait_ge(mixed, 2 * b + 2)
                if bankt is PB and j == 0:
                    pe.wait_ge(relu_done, EC * (b + 1))
                elif bankt is PB:
                    pe.wait_ge(tanh_done, 2 * b + j)
                token_product(xr, r_sb, j, bankt).then_inc(rp_full, 1)

            def value_project(b, j, bankt=PB):
                if j == 0:
                    pe.wait_ge(tanh_done, 2 * (b + 1))
                    pe.wait_ge(act_done, EC * (b + 1))
                    pe.wait_ge(gates_folded, 2 * b + 2)
                elif bankt is PB:
                    pe.wait_ge(y_done, 2 * b + j)
                token_product(ka, cg_sb, j, bankt).then_inc(vp_full, 1)

            def pre_step(b, i, k):
                if i == 0 and k in XNT_AT:
                    xn_transpose(b, XNT_AT.index(k))
                elif k in Q_AT[i]:
                    q_step(b, i, Q_AT[i].index(k))
                elif k in K_AT[i]:
                    k_step(SL * b + i, i, K_AT[i].index(k))
                elif k == V_AT[i]:
                    v_step(SL * b + i, i)

            def post_step(b, p):
                if p in HEADT_AT:
                    head_transpose(b, HEADT_AT.index(p))
                elif p in ATTNT_AT:
                    attn_transpose(b, ATTNT_AT.index(p))
                elif p in OUT_AT:
                    out_project(b, OUT_AT.index(p))
                elif p in XN2T_AT:
                    xn2_transpose(b, XN2T_AT.index(p))
                elif p in KEY_AT:
                    key_project(b, KEY_AT.index(p))
                elif p in REC_AT:
                    receptance_project(b, REC_AT.index(p))
                elif p in VAL_AT:
                    value_project(b, VAL_AT.index(p))

            def prologue():
                for c in range(EC):
                    xn_transpose(0, c, (PA, PB)[c])
                pe.wait_ge(weights_loaded, 16 * 8)
                pe.wait_ge(hT_done, EC)
                project(0, 0, PA, q_full)
                project(0, 1, PB, k_full)
                for j in range(NPC - 1):
                    pe.wait_ge(q_piece, j + 1)
                    take_away(qsp, j, PA, q_full)
                    pe.wait_ge(k_piece, j + 1)
                    take_away(ksp, j, PB, k_full)
                pe.wait_ge(q_piece, NPC)
                project_v(0, PA)
                pe.wait_ge(k_piece, NPC)
                project(1, 0, PB, q_full)
                pe.wait_ge(v_done, 1)
                project(1, 1, PA, k_full)
                for j in range(NPC - 1):
                    pe.wait_ge(q_piece, NPC + j + 1)
                    take_away(qsp, j, PB, q_full)
                    pe.wait_ge(k_piece, NPC + j + 1)
                    take_away(ksp, j, PA, k_full)
                pe.wait_ge(q_piece, SL * NPC)
                project_v(1, PB)
                mod_columns(1, ES[0])
                for k, blk in enumerate((2, 5)):
                    for c in range(EC):
                        last = mm(OT[0:B, k * E:(k + 1) * E], sT[:, c, :], mod_sb[:, c, blk * E:(blk + 1) * E],
                                  start=(c == 0), stop=(c == EC - 1))
                last.then_inc(gate_full, 1)
                for u in range(GS * UM):
                    max_unit(0, 0, u)
                max_transpose(0)
                pe.wait_ge(k_ones_ready, 1)
                pe.wait_ge(v_ones_ready, 1)
                pe.wait_ge(modc_ready, 4)
                pe.wait_ge(gate_step, 1)

            def half(b, par, i, first, last):
                n = SL * b + i
                r, rn = ring(par, i), ring(par, 1) if i == 0 else ring(1 - par, 0)
                for k in range(NPOS):
                    for back, u in exp_units(i, k):
                        if not back or not (first and i == 0):
                            score_unit(n - back, (r - back) % RING, u)
                    if i == 0 or not last:
                        for m in max_units(i, k):
                            max_unit(n + 1, rn, m)
                    if k == PV_BEFORE[i] and not (first and i == 0):
                        pv(n - 1, (r - 1) % RING, 1)
                    if k == PV_THIS[i]:
                        pv(n, r, 0)
                    if not last:
                        pre_step(b + 1, i, k)
                    if k == MAXT_AT[i] and (i == 0 or not last):
                        max_transpose(n + 1)
                    if from_batch(b, 1):
                        post_step(b - 1, NPOS * i + k)
                    if from_batch(b, 2):
                        post_step(b - 2, NPOS * (SL + i) + k)

            def epilogue():
                for k in range(max(EXP_TAIL, POST_TAIL)):
                    if k < EXP_TAIL:
                        score_unit(SL * B - 1, RING - 1, GS * UE - EXP_TAIL + k)
                    post_step(B - 2, NPOS * SL + k)
                pv(SL * B - 1, RING - 1, 1)
                for t in range(TT):
                    head_transpose(B - 1, t, FREE[t])
                for c in range(EC):
                    attn_transpose(B - 1, c, FREE[c])
                for j in range(2):
                    out_project(B - 1, j, FREE[j])
                for c in range(EC):
                    xn2_transpose(B - 1, c, FREE[c])
                for co in range(EC):
                    key_project(B - 1, co, FREE[co])
                for j in range(2):
                    receptance_project(B - 1, j, FREE[2 + j])
                for j in range(2):
                    value_project(B - 1, j, FREE[j])

            slots(pe, prologue, half, epilogue)

        @block.scalar
        def _(act):
            fn = nc.scalar.activation
            act.wait_ge(cond_loaded, 16)
            fn(th_sb, cond_sb, ACT.Tanh, scale=0.5).then_inc(th_ready, 1)

            def norm1(b):
                act.wait_ge(rstd1_ready, b + 1)
                for t in range(TT):
                    last = fn(xin[:, t, :], xin[:, t, :], ACT.Identity, bias=nm1[:, t:t + 1], scale=rs1[:, t:t + 1])
                last.then_inc(xn1_ready, 1)

            def modulate1(b, c, bankt=PA):
                act.wait_ge(xnT_full, EC * b + c + 1)
                act.wait_ge(mpre_loaded, 16 * (b + 1))
                if c == 0:
                    if later(SL * b):
                        act.wait_ge(v_full, SL * b)
                fn(hT[:, c, :], bankt[:, :], ACT.Identity, bias=mpre[:, c:c + 1], scale=mpre[:, EC + c:EC + c + 1])\
                    .then_inc(hT_done, 1)

            def piece(n, which, j, bankt=PA):
                full, done, tile, stored = ((q_full, q_piece, qsp, q_stored) if which == 0 else
                                            (k_full, k_piece, ksp, k_stored))
                act.wait_ge(full, NPC * n + j + 1)
                if j == 0:
                    if later(16 * n):
                        act.wait_ge(stored, 16 * n)
                fn(tile[:, j, :], bankt[:, :], ACT.Copy).then_inc(done, 1)

            def max_piece(n):
                act.wait_ge(mT_full, n + 1)
                if later(16 * n):
                    act.wait_ge(m_stored, 16 * n)
                fn(mT[:, 0, :], MT[0:HS, :], ACT.Copy, scale=-1.0).then_inc(m1_ready, 1)

            def exp_unit(n, u):
                g, v = divmod(u, UE)
                act.wait_ge(sc_full, GS * UE * n + u + 1)
                if v == 0:
                    if later(GS * n + g - 1):
                        act.wait_ge(pv_full, GS * n + g - 1)
                pair, w = divmod(v, 5)
                if w < 4:
                    h, part = 2 * pair + w // 2, w % 2
                    fn(PT[g][:, h, part * T:(part + 1) * T], ES[u % 2][:, :], ACT.Exp, scale=SCALE)\
                        .then_inc(exp_done, 1)
                else:
                    fn(PT[g][:, 2 * pair:2 * pair + 2, 2 * T:HT], ES[u % 2][:, :].rearrange("p (h q) -> p h q", h=2),
                       ACT.Exp, scale=SCALE).then_inc(exp_done, 1)

            def take_pv(n, b, i, g):
                act.wait_ge(pv_full, GS * n + g + 1)
                if later(TT * b):
                    act.wait_ge(oTT_full, TT * b)
                fn(oT[:, GS * i + g, :], OT[:, :], ACT.Copy).then_inc(oT_done, 1)

            def take_attn(b, c, bankt=PB):
                act.wait_ge(aT_full, EC * b + c + 1)
                fn(aT[:, c, :], bankt[:, :], ACT.Copy).then_inc(aT_done, 1)

            def norm2(b):
                act.wait_ge(rstd2_ready, b + 1)
                for t in range(TT):
                    last = fn(attn[:, t, :], x1[:, t, :], ACT.Identity, bias=nm2[:, t:t + 1], scale=rs2[:, t:t + 1])
                last.then_inc(xn2_ready, 1)

            def modulate2(b, c, bankt=PB):
                act.wait_ge(xn2T_full, EC * b + c + 1)
                if later(2 * b):
                    act.wait_ge(mixed, 2 * b)
                fn(h2[:, c, 1:T + 1], bankt[:, :], ACT.Identity, bias=mpost[:, 4 + c:5 + c],
                   scale=mpost[:, 6 + c:7 + c]).then_inc(h2_done, 1)

            def relu(b, c, bankt=PB):
                act.wait_ge(kp_full, EC * b + c + 1)
                if later(2 * b):
                    act.wait_ge(vp_full, 2 * b)
                fn(ka[:, c, :], bankt[:, :], ACT.Relu).then_inc(relu_done, 1)

            def receptance(b, j, bankt=PB):
                act.wait_ge(rp_full, 2 * b + j + 1)
                if later(16 * b):
                    act.wait_ge(out_stored, 16 * b)
                fn(y[:, 2 * j:2 * j + 2, :], bankt[:, :].rearrange("p (t e) -> p t e", t=2), ACT.Tanh, scale=0.5)\
                    .then_inc(tanh_done, 1)

            def pre_step(b, i, k):
                if i == 0 and k in XNT_AT:
                    modulate1(b, XNT_AT.index(k))
                elif k in Q_AT[i] and k != Q_AT[i][1]:
                    piece(SL * b + i, 0, Q_AT[i].index(k))
                elif k in K_AT[i] and k != K_AT[i][1]:
                    piece(SL * b + i, 1, K_AT[i].index(k))

            def post_step(b, p):
                if p in ATTNT_AT:
                    take_attn(b, ATTNT_AT.index(p))
                elif p == NORM2_AT:
                    norm2(b)
                elif p in XN2T_AT:
                    modulate2(b, XN2T_AT.index(p))
                elif p in KEY_AT:
                    relu(b, KEY_AT.index(p))
                elif p in REC_AT:
                    receptance(b, REC_AT.index(p))

            def prologue():
                for c in range(EC):
                    if c == 0:
                        norm1(0)
                    modulate1(0, c, (PA, PB)[c])
                for i in range(SL):
                    for j in (0, 2):
                        piece(i, 0, j, (PA, PB)[i])
                        piece(i, 1, j, (PB, PA)[i])
                norm1(1)
                max_piece(0)

            def half(b, par, i, first, last):
                n = SL * b + i
                for k in range(NPOS):
                    for back, u in exp_units(i, k):
                        if not back or not (first and i == 0):
                            exp_unit(n - back, u)
                    if k == PV_BEFORE[i] and not (first and i == 0):
                        if i == 0:
                            take_pv(n - 1, b - 1, 1, 1)
                        else:
                            take_pv(n - 1, b, 0, 1)
                    if k == PV_THIS[i]:
                        take_pv(n, b, i, 0)
                    if not last:
                        pre_step(b + 1, i, k)
                    if i == 1 and k == NORM1_AT and more(b):
                        norm1(b + 2)
                    if k == MAXT_AT[i] and (i == 0 or not last):
                        max_piece(n + 1)
                    if from_batch(b, 1):
                        post_step(b - 1, NPOS * i + k)
                    if from_batch(b, 2):
                        post_step(b - 2, NPOS * (SL + i) + k)

            def epilogue():
                for k in range(max(EXP_TAIL, POST_TAIL)):
                    if k < EXP_TAIL:
                        exp_unit(SL * B - 1, GS * UE - EXP_TAIL + k)
                    post_step(B - 2, NPOS * SL + k)
                take_pv(SL * B - 1, B - 1, 1, 1)
                for c in range(EC):
                    take_attn(B - 1, c, FREE[c])
                norm2(B - 1)
                for c in range(EC):
                    modulate2(B - 1, c, FREE[c])
                for c in range(EC):
                    relu(B - 1, c, FREE[c])
                for j in range(2):
                    receptance(B - 1, j, FREE[2 + j])

            slots(act, prologue, half, epilogue)

        @block.vector
        def _(dve):
            v = nc.vector
            dve.wait_ge(th_ready, 1)
            v.scalar_tensor_tensor(out=sT, in0=th_sb, scalar=1.0, in1=cond_sb, op0=ALU.add, op1=ALU.mult)\
                .then_inc(silu_ready, 1)
            def stats(b, s, src, st, mv, nw, rs, step, seeded, used):
                if s == 0:
                    if later(b):
                        dve.wait_ge(used, b)
                    for t in range(TT):
                        last = v.bn_stats(st[:, t, :], src[:, t, :])
                    last.then_inc(step, 1)
                elif s == 1:
                    dve.wait_ge(step, 3 * b + 1)
                    v.memset(nw[:, 2, :], 0.0)
                    for t in range(TT):
                        last = v.bn_aggr(mv[:, t, :], st[:, t, :])
                    last.then_inc(step, 1)
                elif s == 2:
                    dve.wait_ge(step, 3 * b + 2)
                    v.tensor_scalar(nw[:, 0, :], mv[:, :, 1], EPS, None, ALU.add).then_inc(step, 1)
                else:
                    dve.wait_ge(step, 3 * b + 3)
                    v.tensor_scalar(nw[:, 1, :], nw[:, 0, :], -0.5, None, ALU.mult)
                    v.tensor_scalar(rs[:, :].bitcast(i32), nw[:, 0, :].bitcast(i32), -0.5, RSQRT_SEED, ALU.mult,
                                    ALU.add).then_inc(seeded, 1)

            def stats1(b, s):
                if s == 0:
                    dve.wait_ge(x_loaded, 16 * (b + 1))
                stats(b, s, xin, st1, mv1, nw1, rs1, stats1_step, seeded1, xn1_ready)

            def piece(n, which, j, bankt=PA):
                full, done, tile = (q_full, q_piece, qsp) if which == 0 else (k_full, k_piece, ksp)
                dve.wait_ge(full, NPC * n + j + 1)
                v.tensor_copy(tile[:, j, :], bankt[:, :]).then_inc(done, 1)

            def take_v(n, r, bankt=PA):
                dve.wait_ge(v_full, n + 1)
                if later(GS * (n - RING + 1)):
                    dve.wait_ge(pv_full, GS * (n - RING + 1))
                v.tensor_copy(Va[r][:, :, :, 0:D], bankt[:, :].rearrange("p (t h d) -> p t h d", t=TT, h=HS))\
                    .then_inc(v_done, 1)

            def max_unit(n, u):
                dve.wait_ge(max_full, GS * UM * n + u + 1)
                if u == 0:
                    if later(n):
                        dve.wait_ge(mT_full, n)
                h0, nh, qb = max_parts(u)
                w = (qb + 1) * P
                v.reduce_max(rmax[:, qb, h0:h0 + nh], MX[u % MXN][:, 0:nh * w].rearrange("p (h k) -> p h k", h=nh),
                             axis=AX.X).then_inc(max_read, 1)

            def max_piece(n):
                dve.wait_ge(m1_ready, n + 1)
                dve.wait_ge(mT_full, n + 1)
                v.scalar_tensor_tensor(out=mT[:, 1, :], in0=MT[0:HS, :], scalar=-1.0, in1=mT[:, 0, :], op0=ALU.mult,
                                       op1=ALU.subtract).then_inc(m2_ready, 1)

            def normalise(b, t, bankt=PB):
                dve.wait_ge(oTT_full, TT * b + t + 1)
                heads = bankt[:, :].rearrange("p (h c) -> p h c", c=CT)
                v.reciprocal(rec[:, t, :], heads[:, :, D]).then_inc(rec_ready, 1)
                dve.wait_ge(rec_ready, TT * b + t + 1)
                if t == 0:
                    if later(EC * b):
                        dve.wait_ge(xn2T_full, EC * b)
                v.tensor_tensor(attn[:, t, :].rearrange("p (h d) -> p h d", d=D), heads[:, :, 0:D],
                                rec[:, t, :].unsqueeze(2).to_broadcast([P, H, D]), ALU.mult).then_inc(attn_done, 1)

            def add_attention(b, j, bankt=PB):
                dve.wait_ge(o_full, 2 * b + j + 1)
                dve.wait_ge(post_loaded, 48 * (b + 1))
                v.tensor_tensor(x1[:, 2 * j:2 * j + 2, :], bankt[:, :].rearrange("p (t e) -> p t e", t=2),
                                x1[:, 2 * j:2 * j + 2, :], ALU.add).then_inc(x1_done, 1)

            def stats2(b, s):
                if s == 0:
                    dve.wait_ge(x1_done, 2 * (b + 1))
                stats(b, s, x1, st2, mv2, nw2, rs2, stats2_step, seeded2, xn2_ready)

            def mix(b, which, dst):
                dve.wait_ge(diff_done, b + 1)
                dve.wait_ge(rp_full, 2 * b)
                for c in range(EC):
                    last = v.scalar_tensor_tensor(out=dst[:, c, :], in0=aT[:, c, :], scalar=mu_sb[:, which, c:c + 1],
                                                  in1=h2[:, c, 0:T], op0=ALU.mult, op1=ALU.add)
                last.then_inc(mixed, 1)

            def gate_value(b, j, bankt=PB):
                dve.wait_ge(vp_full, 2 * b + j + 1)
                dve.wait_ge(tanh_done, 2 * b + j + 1)
                yj = y[:, 2 * j:2 * j + 2, :]
                v.scalar_tensor_tensor(out=yj, in0=yj, scalar=1.0, in1=bankt[:, :].rearrange("p (t e) -> p t e", t=2),
                                       op0=ALU.add, op1=ALU.mult).then_inc(y_done, 1)

            def pre_step(b, i, k, r):
                n = SL * b + i
                if k == Q_AT[i][1]:
                    piece(n, 0, 1)
                elif k == K_AT[i][1]:
                    piece(n, 1, 1)
                elif k == V_AT[i]:
                    take_v(n, r)

            def post_step(b, p):
                if p in HEADT_AT:
                    normalise(b, HEADT_AT.index(p))
                elif p in OUT_AT:
                    add_attention(b, OUT_AT.index(p))
                elif p in STATS2_AT:
                    stats2(b, STATS2_AT.index(p))
                elif p == MIX_AT[0]:
                    mix(b, 1, xk)
                elif p == MIX_AT[1]:
                    mix(b, 0, xr)
                elif p in VAL_AT:
                    gate_value(b, VAL_AT.index(p))

            def take_mod_columns(part, bankt):
                dve.wait_ge(modc_full, part + 1)
                for k in range(2):
                    src = bankt[:, EC * k * B:EC * (k + 1) * B].rearrange("p (c b) -> p b c", c=EC)
                    at = EC * (2 * part + k)
                    v.tensor_scalar(modc[:, :, at:at + EC], src, 0.5, float(k), ALU.mult, ALU.add)\
                        .then_inc(modc_ready, 1)

            def prologue():
                for s in range(4):
                    stats1(0, s)
                take_mod_columns(0, PA)
                dve.wait_ge(modc_ready, 2)
                v.tensor_copy(mpre[:, 0:2 * EC], modc[:, 0, 0:2 * EC]).then_inc(mpre_loaded, 16)
                v.memset(h2[:, :, 0:1], 0.0)
                for r in range(RING):
                    last = v.memset(Va[r][:, :, :, D:CT], 1.0)
                last.then_inc(v_ones_ready, 1)
                for i in range(SL):
                    piece(i, 0, 1, (PA, PB)[i])
                    piece(i, 1, 1, (PB, PA)[i])
                    take_v(i, i, (PA, PB)[i])
                dve.wait_ge(weights_loaded, 16 * 8)
                for s in range(4):
                    stats1(1, s)
                for u in range(GS * UM):
                    max_unit(0, u)
                max_piece(0)
                take_mod_columns(1, ES[0])
                dve.wait_ge(gate_full, 1)
                v.tensor_scalar(gr[0], OT[0:B, :], 0.5, None, ALU.mult).then_inc(gate_step, 1)
                dve.wait_ge(gate_step, 1)
                v.tensor_scalar(gr[1], gr[0], -1.0, None, ALU.mult).then_inc(gate_step, 1)
                dve.wait_ge(gate_step, 2)
                v.scalar_tensor_tensor(out=gr[2], in0=gr[0], scalar=0.25, in1=gr[1], op0=ALU.max, op1=ALU.max)\
                    .then_inc(gate_step, 1)
                dve.wait_ge(gate_step, 3)
                v.tensor_scalar(gr[1], gr[0], 0.0, 2.0, ALU.is_ge, ALU.mult).then_inc(gate_step, 1)
                dve.wait_ge(gate_step, 4)
                v.scalar_tensor_tensor(out=gr[3], in0=gr[1], scalar=-1.0, in1=gr[2], op0=ALU.add, op1=ALU.mult)\
                    .then_inc(gate_step, 1)
                dve.wait_ge(gate_step, 5)
                v.tensor_scalar(gr[3][:, E:2 * E], gr[3][:, E:2 * E], 0.5, None, ALU.mult).then_inc(gate_ready, 1)

            def half(b, par, i, first, last):
                n = SL * b + i
                for k in range(NPOS):
                    if i == 0 or not last:
                        for m in max_units(i, k):
                            max_unit(n + 1, m)
                    if not last:
                        pre_step(b + 1, i, k, ring(1 - par, i))
                    if i == 1 and k in STATS1_AT and more(b):
                        stats1(b + 2, STATS1_AT.index(k))
                    if k == MAXT_AT[i] and (i == 0 or not last):
                        max_piece(n + 1)
                    if from_batch(b, 1):
                        post_step(b - 1, NPOS * i + k)
                    if from_batch(b, 2):
                        post_step(b - 2, NPOS * (SL + i) + k)

            def epilogue():
                for k in range(POST_TAIL):
                    post_step(B - 2, NPOS * SL + k)
                for t in range(TT):
                    normalise(B - 1, t, FREE[t])
                for j in range(2):
                    add_attention(B - 1, j, FREE[j])
                for s in range(4):
                    stats2(B - 1, s)
                mix(B - 1, 1, xk)
                mix(B - 1, 0, xr)
                for j in range(2):
                    gate_value(B - 1, j, FREE[j])

            slots(dve, prologue, half, epilogue)

        @block.gpsimd
        def _(pool):
            g_ = nc.gpsimd
            g_.memset(ident[:, :], 0.0)
            g_.memset(pool_mark[:, :], 0.0)
            g_.memset(newton_c[:, 0, :], 1.5)
            g_.memset(newton_c[:, 1, :], -1.0)
            g_.memset(maskb[:, :], 0.0).then_inc(zeros_ready, 1)
            pool.wait_ge(zeros_ready, 1)
            g_.affine_select(out=ident[:, :], in_=ident[:, :], compare_op=ALU.not_equal, fill=1.0, base=0,
                             pattern=[[-1, P]], channel_multiplier=1).then_inc(ident_ready, 1)
            g_.affine_select(out=maskb[:, :], in_=maskb[:, :], compare_op=ALU.is_ge, fill=NEG, base=0,
                             pattern=[[-1, P]], channel_multiplier=1)
            pool.wait_ge(ident_ready, 1)
            g_.tensor_copy(identb[:, :], ident[:, :])
            g_.tensor_scalar(nidentb[:, :], ident[:, :], -1.0, None, ALU.mult).then_inc(const_ready, 1)

            def mask(n, g):
                pool.wait_ge(exp_done, UE * (GS * n + g + 1))
                g_.tensor_tensor(pool_mark[:, :], pool_mark[:, :], pool_mark[:, :], ALU.mult)
                for kb in range(TT):
                    blk = PT[g][:, :, KBO[kb]:KBO[kb] + P]
                    g_.affine_select(out=blk, in_=blk, compare_op=ALU.is_ge, fill=0.0, base=0,
                                     pattern=[[0, HG], [1, P]], channel_multiplier=-1).then_inc(masked, 1)

            def fold_gates(b):
                pool.wait_ge(post_loaded, 48 * (b + 1))
                if later(2 * b):
                    pool.wait_ge(o_full, 2 * b)
                ga = gate_sb[:, 0:E].unsqueeze(1).to_broadcast([P, EC, E])
                gb = gate_sb[:, E:2 * E].unsqueeze(1).to_broadcast([P, EC, E])
                g_.tensor_tensor(og_sb[:, :, :], o_sb[:, :, :], ga, ALU.mult).then_inc(gates_folded, 1)
                if later(2 * b):
                    pool.wait_ge(vp_full, 2 * b)
                g_.tensor_tensor(cg_sb[:, :, :], c_sb[:, :, :], gb, ALU.mult).then_inc(gates_folded, 1)

            def diff(b):
                pool.wait_ge(h2_done, EC * (b + 1))
                pool.wait_ge(o_full, 2 * (b + 1))
                g_.tensor_tensor(aT[:, :, :], h2[:, :, 1:T + 1], h2[:, :, 0:T], ALU.subtract)\
                    .then_inc(diff_done, 1)

            def square(b, c):
                pool.wait_ge(relu_done, EC * b + c + 1)
                g_.tensor_tensor(ka[:, c, :], ka[:, c, :], ka[:, c, :], ALU.mult).then_inc(act_done, 1)

            def finish(b):
                pool.wait_ge(y_done, 2 * (b + 1))
                g_.tensor_tensor(y[:, :, :], y[:, :, :], x1[:, :, :], ALU.add).then_inc(out_added, 1)
                pool.wait_ge(out_added, b + 1)
                pool.dma_start(out[b].rearrange("(t p) e -> p t e", p=P), y[:, :, :]).then_inc(out_stored, 16)

            def newton(b, mv, nw, rs, nm, seeded, step, ready):
                pool.wait_ge(seeded, b + 1)
                at = NEWTON_STEPS * b
                for _ in range(NEWTON):
                    g_.tensor_tensor(nw[:, 2, :], rs[:, :], rs[:, :], ALU.mult).then_inc(step, 1)
                    pool.wait_ge(step, at + 1)
                    g_.tensor_tensor(nw[:, 3, :], nw[:, 2, :], nw[:, 1, :], ALU.mult).then_inc(step, 1)
                    pool.wait_ge(step, at + 2)
                    g_.tensor_tensor(nw[:, 2, :], nw[:, 3, :], newton_c[:, 0, :], ALU.add).then_inc(step, 1)
                    pool.wait_ge(step, at + 3)
                    g_.tensor_tensor(rs[:, :], rs[:, :], nw[:, 2, :], ALU.mult).then_inc(step, 1)
                    pool.wait_ge(step, at + 4)
                    at = at + 4
                g_.tensor_tensor(nw[:, 3, :], mv[:, :, 0], rs[:, :], ALU.mult).then_inc(step, 1)
                pool.wait_ge(step, at + 1)
                g_.tensor_tensor(nm[:, :], nw[:, 3, :], newton_c[:, 1, :], ALU.mult).then_inc(ready, 1)

            def newton1(b):
                newton(b, mv1, nw1, rs1, nm1, seeded1, newton1_step, rstd1_ready)

            def post_step(b, p):
                if p == STATS2_AT[-1]:
                    newton(b, mv2, nw2, rs2, nm2, seeded2, newton2_step, rstd2_ready)
                if p == FOLD_AT:
                    fold_gates(b)
                if p == DIFF_AT:
                    diff(b)
                if p in KEY_AT:
                    square(b, KEY_AT.index(p))
                if p == VAL_AT[-1]:
                    finish(b)

            def prologue():
                newton1(0)
                pool.wait_ge(rstd1_ready, 1)
                for r in range(RING):
                    last = g_.memset(Ks[r][KQ:KS, :, :], 1.0)
                last.then_inc(k_ones_ready, 1)
                pool.wait_ge(k_ones_ready, 1)
                pool.wait_ge(weights_loaded, 16 * 8)
                newton1(1)

            def half(b, par, i, first, last):
                n = SL * b + i
                for k in range(NPOS):
                    if k == MASK_BEFORE[i] and not (first and i == 0):
                        mask(n - 1, 1)
                    if k == MASK_THIS[i]:
                        mask(n, 0)
                    if i == 1 and k == STATS1_AT[-1] and more(b):
                        newton1(b + 2)
                    if from_batch(b, 1):
                        post_step(b - 1, NPOS * i + k)
                    if from_batch(b, 2):
                        post_step(b - 2, NPOS * (SL + i) + k)

            def epilogue():
                mask(SL * B - 1, 1)
                for k in range(POST_TAIL):
                    post_step(B - 2, NPOS * SL + k)
                for p in range(SL * NPOS):
                    post_step(B - 1, p)

            slots(pool, prologue, half, epilogue)


def sb_view(tile, P, a, n):
    flat = tile[:, :, :].rearrange("p a b -> p (a b)")
    return flat[:, 0:a * n].rearrange("p (a n) -> p a n", a=a)


def bcast_rows(dram, b, P):
    return dram[b].unsqueeze(0).to_broadcast([P, dram.shape[1]])


def max_parts(u):
    g, v = divmod(u, 11)
    if v < 8:
        return 4 * g + v // 2, 1, 3 - v % 2
    if v < 10:
        return 4 * g + 2 * (v - 8), 2, 1
    return 4 * g, 4, 0


def score_parts(u):
    pair, w = divmod(u, 5)
    if w < 4:
        h = 2 * pair + w // 2
        return [(h, 0)] if w % 2 == 0 else [(h, 1), (h, 3)]
    return [(2 * pair, 2), (2 * pair + 1, 2)]


def kernel(**inputs):
    import numpy as _np
    import concourse.bacc as _bacc
    from concourse import mybir as _mybir
    from concourse.bass_utils import run_bass_kernel_spmd as _run

    a = {k: _np.asarray(v) for k, v in inputs.items()}
    E, D, H = 256, 16, 16
    in_w = a["L0_attn_in_proj_weight"].T
    qk = in_w[:, 0:2 * E].reshape(E, 2, 2, H // 2, D).transpose(0, 1, 2, 4, 3).reshape(E, 2 * E)
    arrays = {
        "x": a["L0_attn_query"], "qk_w": qk, "v_w": in_w[:, 2 * E:3 * E], "o_w": a["L0_attn_out_proj_weight"].T,
        "r_w": a["L0_ffn_W_r"].T, "k_w": a["L0_ffn_W_k"].T, "c_w": a["L0_ffn_W_v"].T,
        "mu_r": a["L0_ffn_mu_r"].reshape(2, 128).T, "mu_k": a["L0_ffn_mu_k"].reshape(2, 128).T,
        "cond": a["L0_c"].T, "mod_w": a["L0_wmod"],
    }
    arrays = {k: _np.ascontiguousarray(v) for k, v in arrays.items()}
    nc = _bacc.Bacc("TRN2", target_bir_lowering=False, num_devices=1)
    args = [nc.dram_tensor(k, v.shape, _mybir.dt.from_np(v.dtype), kind="ExternalInput").ap()
            for k, v in arrays.items()]
    out = nc.dram_tensor("out", a["L0_attn_query"].shape, _mybir.dt.float32, kind="ExternalOutput").ap()
    adaln_attention_channel_mix_kernel(nc, *args, out)
    r = _run(nc, [arrays], core_ids=[0])
    return r.results[0]["out"]
```
